# Optimizing a Trainium2 kernel written in Bass

```python
import numpy as np
import jax
import jax.numpy as jnp

def _softmax(x, axis=-1):
    return jax.nn.softmax(x, axis=axis)

def _gelu(x):
    return jax.nn.gelu(x, approximate=True)

def _silu(x):
    return jax.nn.silu(x)

def _sigmoid(x):
    return jax.nn.sigmoid(x)

def _layernorm(x, axis=-1, eps=1e-05):
    m = jnp.mean(x, axis=axis, keepdims=True)
    v = jnp.var(x, axis=axis, keepdims=True)
    return (x - m) / jnp.sqrt(v + eps)

def _scatter_add(tgt, idx, src, axis=0):
    return tgt.at[idx].add(src)

def _segment_sum(src, seg, n):
    return jax.ops.segment_sum(src, seg, n)
kernel_name = 'mk_gnn_ffn_d2_gnn_r32_84ba40'

def setup_inputs(seed: int=0):
    np.random.seed(seed)
    _w = jnp.asarray

    def _rec_inputs():
        import jax
        import jax.numpy as jnp
        _gk = jax.random.key(seed)
        x = -0.0002117 + 1 * jax.random.normal(jax.random.fold_in(_gk, 1), (3125, 256), jnp.float32)
        src = jax.random.randint(jax.random.fold_in(_gk, 2), (50000,), 0, 3125, jnp.int32)
        dst = jax.random.randint(jax.random.fold_in(_gk, 3), (50000,), 0, 3125, jnp.int32)
        _o = jnp.argsort(dst, stable=True)
        src = src[_o]
        dst = dst[_o]
        edge_attr_3 = -1.09012e-05 + 0.99985 * jax.random.normal(jax.random.fold_in(_gk, 12), (50000, 3), jnp.float32)
        edge_weight = jax.random.uniform(jax.random.fold_in(_gk, 14), (50000,), jnp.float32, 0.0, 1)
        return (x, src, dst, edge_attr_3, edge_weight)
    x, src, dst, edge_attr_3, edge_weight = _rec_inputs()

    def _L0_gnn_setup():
        import jax, jax.numpy as jnp
        import numpy as np
        N_NODES = 3125
        key = jax.random.key(seed)
        k = jax.random.split(key, 7)
        N, E, F_IN, F_OUT = (N_NODES, 100000, 256, 256)
        stdv = 1.0 / np.sqrt(F_OUT)
        return {'x': jax.random.normal(k[0], (N, F_IN), dtype=jnp.float32), 'edge_row': jax.random.randint(k[1], (E,), 0, N, dtype=jnp.int32), 'edge_col': jax.random.randint(k[2], (E,), 0, N, dtype=jnp.int32), 'edge_val': jax.random.uniform(k[3], (E,), dtype=jnp.float32), 'weight': jax.random.uniform(k[4], (F_IN, F_OUT), dtype=jnp.float32, minval=-stdv, maxval=stdv), 'learnable_diag': 0.01 * jax.random.normal(k[5], (F_IN,), dtype=jnp.float32), 'bias': jax.random.uniform(k[6], (F_OUT,), dtype=jnp.float32, minval=-stdv, maxval=stdv)}
    _L0_gnn_all = _L0_gnn_setup()
    _L0_gnn_in = {k: v for k, v in _L0_gnn_all.items() if k in ('weight', 'learnable_diag', 'bias')}
    del _L0_gnn_all

    def _L0_ffn_setup():
        import jax, jax.numpy as jnp
        import numpy as np
        B, S, H, F, E, K = (8, 128, 256, 512, 16, 2)
        EPS = 1e-05
        key = jax.random.key(seed)
        ks = jax.random.split(key, 9)
        sc = 0.02
        return {'x': jax.random.normal(ks[0], (B, S, H), dtype=jnp.float32), 'gate_w': jax.random.normal(ks[1], (H, E), dtype=jnp.float32) * sc, 'gate_b': jnp.zeros((E,), dtype=jnp.float32), 'w1': jax.random.normal(ks[2], (E, H, F), dtype=jnp.float32) * sc, 'b1': jnp.zeros((E, F), dtype=jnp.float32), 'w2': jax.random.normal(ks[3], (E, F, H), dtype=jnp.float32) * sc, 'b2': jnp.zeros((E, H), dtype=jnp.float32), 'gamma': jnp.ones((H,), dtype=jnp.float32), 'beta': jnp.zeros((H,), dtype=jnp.float32)}
    _L0_ffn_all = _L0_ffn_setup()
    _L0_ffn_in = {k: v for k, v in _L0_ffn_all.items() if k in ('gate_w', 'gate_b', 'w1', 'b1', 'w2', 'b2', 'gamma', 'beta')}
    del _L0_ffn_all

    def _L1_gnn_setup():
        import jax, jax.numpy as jnp
        import numpy as np
        N = 50000
        E = 12500
        IN = 256
        H = 8
        D = 32
        EF = 3
        key = jax.random.key(seed)
        ks = jax.random.split(key, 8)
        x = jax.random.normal(ks[0], (N, IN), dtype=jnp.float32)
        edge_index = jax.random.randint(ks[1], (2, E), 0, N, dtype=jnp.int64)
        edge_attr = jax.random.normal(ks[2], (E, EF), dtype=jnp.float32)
        W = jax.random.normal(ks[3], (H * D, IN), dtype=jnp.float32) * np.float32(np.sqrt(2.0 / (IN + H * D)))
        a_src = jax.random.normal(ks[4], (H, D), dtype=jnp.float32) * np.float32(np.sqrt(2.0 / (H + D)))
        a_dst = jax.random.normal(ks[5], (H, D), dtype=jnp.float32) * np.float32(np.sqrt(2.0 / (H + D)))
        edge_W = jax.random.normal(ks[6], (H * D, EF), dtype=jnp.float32) * np.float32(np.sqrt(2.0 / (EF + H * D)))
        edge_b = jnp.zeros((H * D,), dtype=jnp.float32)
        bias = jnp.zeros((H * D,), dtype=jnp.float32)
        return {'x': x, 'W': W, 'a_src': a_src, 'a_dst': a_dst, 'edge_W': edge_W, 'edge_b': edge_b, 'bias': bias, 'edge_attr': edge_attr, 'edge_index': edge_index}
    _L1_gnn_all = _L1_gnn_setup()
    _L1_gnn_in = {k: v for k, v in _L1_gnn_all.items() if k in ('W', 'a_src', 'a_dst', 'edge_W', 'edge_b', 'bias')}
    del _L1_gnn_all

    def _L1_ffn_setup():
        import jax, jax.numpy as jnp
        import numpy as np
        C = 256
        HID = 1024
        E = 8
        TEMP = 1.0
        key = jax.random.key(seed)
        ks = jax.random.split(key, 7)
        x = jax.random.normal(ks[0], (8, 512, C), dtype=jnp.float32)
        W1 = jax.random.normal(ks[1], (C, HID), dtype=jnp.float32) * 0.02
        b1 = jnp.zeros((HID,), dtype=jnp.float32)
        Wg = jax.random.normal(ks[2], (HID, E), dtype=jnp.float32) * 0.02
        bg = jnp.zeros((E,), dtype=jnp.float32)
        Wd = jax.random.normal(ks[3], (E, HID, C), dtype=jnp.float32) * 0.02
        bd = jnp.zeros((E, C), dtype=jnp.float32)
        return {'x': x, 'W1': W1, 'b1': b1, 'Wg': Wg, 'bg': bg, 'Wd': Wd, 'bd': bd}
    _L1_ffn_all = _L1_ffn_setup()
    _L1_ffn_in = {k: v for k, v in _L1_ffn_all.items() if k in ('W1', 'b1', 'Wg', 'bg', 'Wd', 'bd')}
    del _L1_ffn_all
    return {'x': x, 'src': src, 'dst': dst, 'edge_attr_3': edge_attr_3, 'edge_weight': edge_weight, 'L0_gnn_weight': _L0_gnn_in['weight'], 'L0_gnn_learnable_diag': _L0_gnn_in['learnable_diag'], 'L0_gnn_bias': _L0_gnn_in['bias'], 'L0_ffn_gate_w': _L0_ffn_in['gate_w'], 'L0_ffn_gate_b': _L0_ffn_in['gate_b'], 'L0_ffn_w1': _L0_ffn_in['w1'], 'L0_ffn_b1': _L0_ffn_in['b1'], 'L0_ffn_w2': _L0_ffn_in['w2'], 'L0_ffn_b2': _L0_ffn_in['b2'], 'L0_ffn_gamma': _L0_ffn_in['gamma'], 'L0_ffn_beta': _L0_ffn_in['beta'], 'L1_gnn_W': _L1_gnn_in['W'], 'L1_gnn_a_src': _L1_gnn_in['a_src'], 'L1_gnn_a_dst': _L1_gnn_in['a_dst'], 'L1_gnn_edge_W': _L1_gnn_in['edge_W'], 'L1_gnn_edge_b': _L1_gnn_in['edge_b'], 'L1_gnn_bias': _L1_gnn_in['bias'], 'L1_ffn_W1': _L1_ffn_in['W1'], 'L1_ffn_b1': _L1_ffn_in['b1'], 'L1_ffn_Wg': _L1_ffn_in['Wg'], 'L1_ffn_bg': _L1_ffn_in['bg'], 'L1_ffn_Wd': _L1_ffn_in['Wd'], 'L1_ffn_bd': _L1_ffn_in['bd']}

def reference(x, src, dst, edge_attr_3, edge_weight, L0_gnn_weight, L0_gnn_learnable_diag, L0_gnn_bias, L0_ffn_gate_w, L0_ffn_gate_b, L0_ffn_w1, L0_ffn_b1, L0_ffn_w2, L0_ffn_b2, L0_ffn_gamma, L0_ffn_beta, L1_gnn_W, L1_gnn_a_src, L1_gnn_a_dst, L1_gnn_edge_W, L1_gnn_edge_b, L1_gnn_bias, L1_ffn_W1, L1_ffn_b1, L1_ffn_Wg, L1_ffn_bg, L1_ffn_Wd, L1_ffn_bd):
    import jax
    import jax.numpy as jnp

    def _L0_gnn_ref(x, edge_row, edge_col, edge_val, weight, learnable_diag, bias):
        import jax, jax.numpy as jnp
        import numpy as np
        N_NODES = 3125
        gathered = edge_val[:, None] * x[edge_col]
        e1 = jax.ops.segment_sum(gathered, edge_row, num_segments=N_NODES)
        e2 = e1 * (learnable_diag + 1.0)
        e4 = x - e2
        out = e4 @ weight + bias
        return out

    def _L0_ffn_ref(x, gate_w, gate_b, w1, b1, w2, b2, gamma, beta):
        import jax, jax.numpy as jnp
        import numpy as np
        B, S, H, F, E, K = (8, 128, 256, 512, 16, 2)
        EPS = 1e-05
        gate_logits = x @ gate_w + gate_b
        topk_vals, topk_idx = jax.lax.top_k(gate_logits, K)
        topk_w = jax.nn.softmax(topk_vals, axis=-1)
        h = jax.nn.relu(jnp.einsum('bsh,ehf->bsef', x, w1) + b1)
        expert_out = jnp.einsum('bsef,efh->bseh', h, w2) + b2
        sel = jnp.take_along_axis(expert_out, topk_idx[:, :, :, None], axis=2)
        moe = jnp.sum(topk_w[..., None] * sel, axis=2)
        y = x + moe
        mu = jnp.mean(y, axis=-1, keepdims=True)
        var = jnp.var(y, axis=-1, keepdims=True)
        return (y - mu) / jnp.sqrt(var + EPS) * gamma + beta

    def _L1_gnn_ref(x, W, a_src, a_dst, edge_W, edge_b, bias, edge_attr, edge_index):
        import jax, jax.numpy as jnp
        import numpy as np
        N = 50000
        E = 12500
        IN = 256
        H = 8
        D = 32
        EF = 3
        n = x.shape[0]
        h = (x @ W.T).reshape(n, H, D)
        src, dst = (edge_index[0], edge_index[1])
        h_src = h[src]
        h_dst = h[dst]
        alpha = jnp.einsum('ehd,hd->eh', h_src, a_src) + jnp.einsum('ehd,hd->eh', h_dst, a_dst)
        enc = jax.nn.relu(edge_attr @ edge_W.T + edge_b).reshape(-1, H, D)
        alpha = alpha + jnp.sum(enc * h_dst, axis=-1)
        alpha = jnp.where(alpha >= 0, alpha, 0.2 * alpha)
        amax = jax.ops.segment_max(alpha, dst, num_segments=n)
        ex = jnp.exp(alpha - amax[dst])
        denom = jax.ops.segment_sum(ex, dst, num_segments=n)
        attn = ex / jnp.maximum(denom[dst], 1e-10)
        out = jax.ops.segment_sum(h_src * attn[..., None], dst, num_segments=n)
        return out.reshape(n, H * D) + bias

    def _L1_ffn_ref(x, W1, b1, Wg, bg, Wd, bd):
        import jax, jax.numpy as jnp
        import numpy as np
        C = 256
        HID = 1024
        E = 8
        TEMP = 1.0
        orig_shape = x.shape
        xf = x.reshape(-1, orig_shape[-1])
        H = jax.nn.gelu(xf @ W1 + b1, approximate=False)
        probs = jax.nn.softmax((H @ Wg + bg) / TEMP, axis=-1)
        assign = jnp.argmax(probs, axis=-1)
        out = jnp.zeros_like(xf)
        for e in range(Wd.shape[0]):
            y = H @ Wd[e] + bd[e]
            sel = (assign == e)[:, None]
            out = out + jnp.where(sel, probs[:, e:e + 1] * y, 0.0)
        return out.reshape(orig_shape)
    edge_index = jnp.stack([src, dst])
    x = x + _L0_gnn_ref(_layernorm(x, axis=-1), src, dst, edge_weight, L0_gnn_weight, L0_gnn_learnable_diag, L0_gnn_bias)
    x = x + _L0_ffn_ref(_layernorm(x, axis=-1)[None], L0_ffn_gate_w, L0_ffn_gate_b, L0_ffn_w1, L0_ffn_b1, L0_ffn_w2, L0_ffn_b2, L0_ffn_gamma, L0_ffn_beta)[0]
    x = x + _L1_gnn_ref(_layernorm(x, axis=-1), L1_gnn_W, L1_gnn_a_src, L1_gnn_a_dst, L1_gnn_edge_W, L1_gnn_edge_b, L1_gnn_bias, edge_attr_3, edge_index)
    x = x + _L1_ffn_ref(_layernorm(x, axis=-1)[None], L1_ffn_W1, L1_ffn_b1, L1_ffn_Wg, L1_ffn_bg, L1_ffn_Wd, L1_ffn_bd)[0]
    return x

_drawn_inputs = setup_inputs


def setup_inputs(seed=0):
    import zlib

    import numpy as np

    out = dict(_drawn_inputs(seed))
    spreads = {'L0_ffn_gate_b': (0.0, 0.317),
     'L0_ffn_b1': (0.0, 0.8),
     'L0_ffn_b2': (0.0, 0.297),
     'L0_ffn_gamma': (1.0, 0.2),
     'L0_ffn_beta': (0.0, 0.1),
     'L1_gnn_edge_b': (0.0, 0.371),
     'L1_gnn_bias': (0.0, 0.1),
     'L1_ffn_b1': (0.0, 0.8),
     'L1_ffn_bg': (0.0, 0.8),
     'L1_ffn_bd': (0.0, 0.8)}
    factors = {'L0_gnn_learnable_diag': 6.414, 'L1_ffn_W1': 7.327, 'L1_ffn_Wg': 7.704, 'L1_ffn_Wd': 8.0}
    for name, (base, spread) in spreads.items():
        noise = np.random.default_rng([zlib.crc32(name.encode()), seed]).standard_normal(out[name].shape)
        drawn = base * np.exp(spread * noise) if base else spread * noise
        out[name] = jnp.asarray(drawn.astype(out[name].dtype))
    for name, factor in factors.items():
        out[name] = (out[name] * factor).astype(out[name].dtype)
    return out
```

```python
import concourse.bass as bass
from concourse import mybir
from concourse.alu_op_type import AluOpType as ALU
from contextlib import ExitStack, contextmanager

F32 = mybir.dt.float32
I32 = mybir.dt.int32
BF16 = mybir.dt.bfloat16
ACT = mybir.ActivationFunctionType
AX = mybir.AxisListType.X

P = 128
N = 3125
C = 256
KC = C // P
NT = (N + P - 1) // P
NPAD = NT * P
E = 50000
EP, EJ = 125, 400
G = 4
GE = G * P
NG = (E + NT * (GE - 1)) // GE
H, D = 8, 32
E0, F0 = 16, 512
E1, F1 = 8, 1024
FC0, FC1 = F0 // P, F1 // P
S0 = (2 * NPAD + E0 * (P - 1)) // P
S1 = (NPAD + E1 * (P - 1)) // P
EPS = 1e-5
BIG = 2.0 ** 100


class Chain:

    def __init__(self, eng, sem):
        self.eng, self.sem, self.base, self.n = eng, sem, 0, 0

    def __call__(self, ins):
        self.n += 1
        ins.then_inc(self.sem, 1)
        self.eng.wait_ge(self.sem, self.base + self.n)

    def turn(self, i, per):
        self.start, self.per = (self.base + self.n if not hasattr(self, "start") else self.start), per
        self.base, self.n = self.start + i * per, 0

    def end(self, turns):
        assert self.n == self.per, (self.n, self.per)
        self.base, self.n = self.start + turns * self.per, 0
        del self.start


class Pool_:

    def __init__(self, nc, ctx, tag):
        self.nc, self.ctx, self.tag = nc, ctx, tag

    def sb(self, name, shape, dt=F32):
        return self.ctx.enter_context(self.nc.sbuf_tensor(f"{self.tag}_{name}", shape, dt))

    def ps(self, name, shape, dt=F32):
        return self.ctx.enter_context(self.nc.psum_tensor(f"{self.tag}_{name}", shape, dt))

    def sem(self, name):
        sem = self.nc.alloc_semaphore(f"{self.tag}_{name}")
        self.ctx.callback(spent.append, sem)
        return sem


spent = []


def reuse_semaphores(nc):
    nc.clear_and_free_semaphores(list(spent))
    spent.clear()
    nc.all_engine_barrier()


def bc(ap, at, n):
    shape = list(ap.shape)
    ap = ap.unsqueeze(at)
    return ap.broadcast_to(shape[:at] + [n] + shape[at:])


@contextmanager
def guarded(eng, only_if):
    if only_if is None:
        yield
    else:
        flag = eng.value_load(only_if, min_val=0, max_val=P)
        with eng.If(flag > 0):
            yield


def sort_positions(nc, tag, cst, key, PK, J, K, unit, pos, ngroups, group_bucket, only_if=None):
    shift = unit.bit_length() - 1
    with ExitStack() as ctx:
        a = Pool_(nc, ctx, tag)
        mask = a.sb("mask", [P, K, J])
        seen = a.sb("seen", [P, K, J])
        before = a.sb("before", [P, K])
        count = a.sb("count", [P, K])
        ti = a.sb("ti", [P, K], I32)
        groups = a.sb("groups", [P, K])
        ends = a.sb("ends", [P, K])
        base = a.sb("base", [P, K])
        posf = a.sb("posf", [P, J])
        cmp = a.sb("cmp", [1, ngroups, K])
        gbf = a.sb("gbf", [1, ngroups])
        below_ps = a.ps("below", [P, 512])
        total_ps = a.ps("total", [P, 512])
        s_chain, s_count, s_sums = a.sem("chain"), a.sem("count"), a.sem("sums")
        with nc.Block() as block:

            @block.vector
            def _(dve):
                with guarded(dve, only_if):
                    link = Chain(dve, s_chain)
                    V = nc.vector
                    link(V.tensor_tensor(mask[:PK], bc(key, 1, K), bc(cst["iota"][:PK, 0:K], 2, J), ALU.is_equal))
                    flat = mask[:PK].rearrange("p k j -> p (k j)")
                    link(V.tensor_tensor_scan(seen[:PK].rearrange("p k j -> p (k j)"), flat, flat, 0.0, ALU.add, ALU.max))
                    link(V.memset(before[:PK, 0:1], 0.0))
                    link(V.tensor_copy(before[:PK, 1:K], seen[:PK, 0:K - 1, J - 1]))
                    V.tensor_tensor(count[:PK], seen[:PK, :, J - 1], before[:PK], ALU.subtract).then_inc(s_count, 1)
                    dve.wait_ge(s_sums, 1)
                    link(V.tensor_scalar(ti[:], total_ps[:, 0:K], float(unit - 1), None, ALU.add))
                    link(V.tensor_scalar(ti[:], ti[:], shift, None, ALU.arith_shift_right))
                    link(V.tensor_copy(groups[:], ti[:]))
                    link(V.tensor_tensor_scan(ends[:], groups[:], groups[:], 0.0, ALU.add, ALU.max))
                    link(V.tensor_tensor(base[:], ends[:], groups[:], ALU.subtract))
                    link(V.tensor_scalar(base[:], base[:], float(unit), -1.0, ALU.mult, ALU.add))
                    link(V.tensor_tensor(base[:PK], base[:PK], before[:PK], ALU.subtract))
                    link(V.tensor_tensor(base[:PK], base[:PK], below_ps[:PK, 0:K], ALU.add))
                    link(V.tensor_tensor(seen[:PK], seen[:PK], bc(base[:PK], 2, J), ALU.add))
                    link(V.tensor_tensor(seen[:PK], seen[:PK], mask[:PK], ALU.mult))
                    link(V.tensor_reduce(posf[:PK], seen[:PK].rearrange("p k j -> p j k"), AX, ALU.add))
                    link(V.tensor_copy(pos, posf[:PK]))
                    link(V.tensor_tensor(cmp[:], bc(cst["iota"][0:1, 0:ngroups], 2, K), bc(ends[0:1], 1, ngroups), ALU.is_ge))
                    link(V.tensor_reduce(gbf[:], cmp[:], AX, ALU.add))
                    link(V.tensor_scalar(group_bucket, gbf[:], float(K - 1), None, ALU.min))

            @block.tensor
            def _(pe):
                with guarded(pe, only_if):
                    pe.wait_ge(s_count, 1)
                    nc.tensor.matmul(below_ps[:, 0:K], cst["lower"][:PK, :], count[:PK], start=True, stop=True)
                    nc.tensor.matmul(total_ps[:, 0:K], cst["ones"][:PK, :], count[:PK], start=True, stop=True).then_inc(s_sums, 1)


def scatter_rows(nc, tag, pos, rows, table, PK, turns, B, clear=None, slots=2, only_if=None):
    R = rows.shape[2]
    with ExitStack() as ctx:
        a = Pool_(nc, ctx, tag)
        ix = [a.sb(f"ix{s}", [P, B], I32) for s in range(slots)]
        rw = [a.sb(f"rw{s}", [P, B, R], rows.dtype) for s in range(slots)]
        s_full = [a.sem(f"full{s}") for s in range(slots)]
        s_free = [a.sem(f"free{s}") for s in range(slots)]
        s_clear, s_begin = a.sem("clear"), a.sem("begin")
        with nc.Block() as block:

            @block.sync
            def _(sp):
                with guarded(sp, only_if):
                    if clear is not None:
                        sp.dma_start(clear[0], clear[1]).then_inc(s_clear, 16)
                        sp.wait_ge(s_clear, 16)

            @block.vector
            def _(dve):
                with guarded(dve, only_if):
                    def fill_slots(i, first=False):
                        for s in range(slots):
                            if not first:
                                dve.wait_ge(s_free[s], i * (16 * B))
                            at = i * (slots * B) + s * B
                            nc.vector.tensor_copy(ix[s][:PK], pos[:, bass.ds(at, B)]).then_inc(s_full[s], 1)
                            nc.vector.tensor_copy(rw[s][:PK], rows[:, bass.ds(at, B), :]).then_inc(s_full[s], 1)

                    fill_slots(0, first=True)
                    with dve.Fori(1, turns) as i:
                        fill_slots(i)

            @block.gpsimd
            def _(pool):
                with guarded(pool, only_if):
                    if clear is not None:
                        pool.wait_ge(s_clear, 16)
                    with pool.Fori(0, turns) as i:
                        for s in range(slots):
                            pool.wait_ge(s_full[s], (i + 1) * 2)
                            pool.sem_inc(s_begin, 1)
                            for b in range(B):
                                nc.gpsimd.indirect_dma_start(
                                    table, bass.IndirectOffsetOnAxis(ap=ix[s][:PK, b:b + 1], axis=0),
                                    rw[s][:PK, b, :], None).then_inc(s_free[s], 16)
                    for s in range(slots):
                        pool.wait_ge(s_free[s], 16 * B * turns)


def constants(nc, a, cst):
    it, ip = a.sb("it", [P, P]), a.sb("ip", [P, 1])
    s_pool, s_chain = a.sem("pool"), a.sem("chain")
    with nc.Block() as block:

        @block.gpsimd
        def _(pool):
            nc.gpsimd.iota(cst["iota"][:], pattern=[[1, P]], base=0, channel_multiplier=0,
                           allow_small_or_imprecise_dtypes=True).then_inc(s_pool, 1)
            nc.gpsimd.iota(ip[:], pattern=[[0, 1]], base=0, channel_multiplier=1,
                           allow_small_or_imprecise_dtypes=True).then_inc(s_pool, 1)

        @block.vector
        def _(dve):
            link = Chain(dve, s_chain)
            dve.wait_ge(s_pool, 2)
            link(nc.vector.tensor_scalar(cst["lower"][:], cst["iota"][:], ip[:, 0:1], None, ALU.is_gt))
            link(nc.vector.tensor_scalar(cst["ident"][:], cst["iota"][:], ip[:, 0:1], None, ALU.is_equal))
            link(nc.vector.tensor_copy(cst["identb"][:], cst["ident"][:]))
            link(nc.vector.memset(cst["ones"][:], 1.0))
            link(nc.vector.memset(it[:], 0.0))


def edge_keys(nc, a, A, cst, ek, rec0, rec1, unsorted):
    src, dst = a.sb("src", [P, EJ], I32), a.sb("dst", [P, EJ], I32)
    w, attr = a.sb("w", [P, EJ]), a.sb("attr", [P, EJ, 3])
    part = a.sb("part", [P, EJ], I32)
    nxt, falls, falls_ps = a.sb("nxt", [P, EJ], I32), a.sb("falls", [P, 1]), a.ps("falls_ps", [P, 512])
    s_in, s_chain, s_next, s_falls, s_sum, s_clear = (a.sem(m) for m in ("in", "chain", "next", "falls", "sum", "clear"))
    with nc.Block() as block:

        @block.gpsimd
        def _(pool):
            nc.gpsimd.memset(nxt[:], N).then_inc(s_clear, 1)

        @block.sync
        def _(sp):
            for to, of in ((src, A["src"]), (dst, A["dst"]), (w, A["edge_weight"])):
                sp.dma_start(to[:EP], of.rearrange("(p j) -> p j", p=EP)).then_inc(s_in, 16)
            sp.dma_start(attr[:EP], A["edge_attr_3"].rearrange("(p j) c -> p j c", p=EP)).then_inc(s_in, 16)
            sp.wait_ge(s_clear, 1)
            last = (EP - 1) * EJ
            sp.dma_start(nxt[0:EP - 1], A["dst"][1:last + 1].rearrange("(p j) -> p j", j=EJ)).then_inc(s_next, 16)
            sp.dma_start(nxt[EP - 1:EP, 0:EJ - 1], A["dst"][last + 1:E].unsqueeze(0)).then_inc(s_next, 16)

        @block.vector
        def _(dve):
            link = Chain(dve, s_chain)
            V = nc.vector
            dve.wait_ge(s_in, 64)
            for k, (near, far, rec) in enumerate(((src, dst, rec0), (dst, src, rec1))):
                link(V.tensor_scalar(part[:EP], near[:EP], 7, None, ALU.arith_shift_right))
                link(V.tensor_copy(ek[k][:EP], part[:EP]))
                link(V.tensor_scalar(part[:EP], near[:EP], P - 1, None, ALU.bitwise_and))
                link(V.tensor_copy(rec[:EP, :, 1], part[:EP]))
                link(V.tensor_copy(rec[:EP, :, 0], far[:EP]))
            link(V.tensor_copy(rec0[:EP, :, 2], w[:EP]))
            link(V.memset(rec0[:EP, :, 3], 0.0))
            link(V.tensor_copy(rec1[:EP, :, 2:5], attr[:EP]))
            link(V.memset(rec1[:EP, :, 5], 1.0))
            link(V.tensor_copy(rec1[:EP, :, 6], ek[1][:EP]))
            link(V.memset(rec1[:EP, :, 7], 0.0))
            dve.wait_ge(s_next, 32)
            link(V.tensor_tensor(part[:EP], dst[:EP], nxt[:EP], ALU.is_gt))
            link(V.tensor_copy(w[:EP], part[:EP]))
            V.tensor_reduce(falls[:EP], w[:EP], AX, ALU.max).then_inc(s_falls, 1)
            dve.wait_ge(s_sum, 1)
            link(V.tensor_copy(unsorted[:], falls_ps[0:1, 0:1]))

        @block.tensor
        def _(pe):
            pe.wait_ge(s_falls, 1)
            nc.tensor.matmul(falls_ps[0:1, 0:1], cst["ones"][:EP, 0:1], falls[:EP], start=True, stop=True).then_inc(s_sum, 1)


def order_places(nc, cst, key, rec, pos, unsorted):
    tmp = nc.dram_tensor("places", (E, 8), F32, kind="Internal").ap()
    only_if = unsorted[0:1, 0:1]
    for shift, K in ((0, 16), (4, 8)):
        with ExitStack() as ctx:
            a = Pool_(nc, ctx, f"place{shift}")
            part, digit = a.sb("part", [P, EJ], I32), a.sb("digit", [P, EJ])
            s_chain, s_back = a.sem("chain"), a.sem("back")
            with nc.Block() as block:

                @block.vector
                def _(dve):
                    link, V = Chain(dve, s_chain), nc.vector
                    link(V.tensor_copy(part[:EP], rec[:EP, :, 1]))
                    link(V.tensor_scalar(part[:EP], part[:EP], shift, K - 1, ALU.arith_shift_right, ALU.bitwise_and))
                    link(V.tensor_copy(digit[:EP], part[:EP]))

            sort_positions(nc, f"psort{shift}", cst, digit[:EP], EP, EJ, K, 1, pos[:EP], 1, part[0:1, 0:1], only_if=only_if)
            scatter_rows(nc, f"pscat{shift}", pos[:EP], rec[:EP], tmp, EP, 25, 8, only_if=only_if)
            with nc.Block() as block:

                @block.sync
                def _(sp):
                    with guarded(sp, only_if):
                        sp.dma_start(rec[:EP], tmp.rearrange("(p j) r -> p j r", p=EP)).then_inc(s_back, 16)
                        sp.wait_ge(s_back, 16)

            with nc.Block() as block:

                @block.vector
                def _(dve):
                    nc.vector.tensor_copy(key[:EP], rec[:EP, :, 6]).then_inc(s_chain, 1)


def load_sorted(nc, a, tables, tiles):
    s_in = a.sem("in")
    with nc.Block() as block:

        @block.sync
        def _(sp):
            for t, (table, tile) in enumerate(zip(tables, tiles)):
                sp.dma_start(tile[:], table.rearrange("(g p q) r -> p g (q r)", p=P, q=G)).then_inc(s_in, 16)
            sp.wait_ge(s_in, 16 * len(tables))



TB = 5
TURNS = NT // TB
HW = H * (D + 1)
HR = HW + H
HN = C + H
PF = 10


def load_nodes(nc, a, x_dram, x):
    s_zero, s_in = a.sem("zero"), a.sem("in")
    full = (NT - 1) * P
    with nc.Block() as block:

        @block.vector
        def _(dve):
            nc.vector.memset(x[:, NT - 1, :], 0.0).then_inc(s_zero, 1)

        @block.sync
        def _(sp):
            sp.dma_start(x[:, 0:NT - 1, :], x_dram[0:full].rearrange("(t p) c -> p t c", p=P)).then_inc(s_in, 16)
            sp.wait_ge(s_zero, 1)
            sp.dma_start(x[0:N - full, NT - 1, :], x_dram[full:N]).then_inc(s_in, 16)
            sp.wait_ge(s_in, 32)


def store_nodes(nc, a, x, x_dram):
    s_out = a.sem("out")
    full = (NT - 1) * P
    with nc.Block() as block:

        @block.sync
        def _(sp):
            sp.dma_start(x_dram[0:full].rearrange("(t p) c -> p t c", p=P), x[:, 0:NT - 1, :]).then_inc(s_out, 16)
            sp.dma_start(x_dram[full:N], x[0:N - full, NT - 1, :]).then_inc(s_out, 16)
            sp.wait_ge(s_out, 32)


def layernorm(nc, tag, x, y, table=None):
    with ExitStack() as ctx:
        a = Pool_(nc, ctx, tag)
        st = a.sb("st", [P, NT, 6])
        mean, var, t0 = a.sb("mean", [P, NT]), a.sb("var", [P, NT]), a.sb("t0", [P, NT])
        s_stats, s_chain, s_var, s_std = a.sem("stats"), a.sem("chain"), a.sem("var"), a.sem("std")
        s_y, s_out = a.sem("y"), a.sem("out")
        with nc.Block() as block:

            @block.vector
            def _(dve):
                link, V = Chain(dve, s_chain), nc.vector
                with dve.Fori(0, NT) as t:
                    V.bn_stats(st[:, bass.ds(t, 1), :].rearrange("p a b -> p (a b)"),
                               x[:, bass.ds(t, 1), :].rearrange("p a b -> p (a b)")).then_inc(s_stats, 1)
                dve.wait_ge(s_stats, NT)
                link(V.tensor_tensor(mean[:], st[:, :, 1], st[:, :, 4], ALU.add))
                link(V.tensor_scalar(mean[:], mean[:], 0.5, None, ALU.mult))
                link(V.tensor_tensor(var[:], st[:, :, 1], st[:, :, 4], ALU.subtract))
                link(V.tensor_tensor(var[:], var[:], var[:], ALU.mult))
                link(V.tensor_tensor(t0[:], st[:, :, 2], st[:, :, 5], ALU.add))
                link(V.tensor_scalar(t0[:], t0[:], 1.0 / C, EPS, ALU.mult, ALU.add))
                V.scalar_tensor_tensor(var[:], var[:], 0.25, t0[:], ALU.mult, ALU.add).then_inc(s_var, 1)
                dve.wait_ge(s_std, 1)
                link(V.reciprocal(t0[:], t0[:]))
                with dve.Fori(0, NT) as t:
                    V.tensor_scalar(y[:, bass.ds(t, 1), :].rearrange("p a b -> p (a b)"),
                                    x[:, bass.ds(t, 1), :].rearrange("p a b -> p (a b)"),
                                    mean[:, bass.ds(t, 1)], t0[:, bass.ds(t, 1)],
                                    ALU.subtract, ALU.mult).then_inc(s_y, 1)

            @block.scalar
            def _(act):
                act.wait_ge(s_var, 1)
                nc.scalar.activation(t0[:], var[:], ACT.Sqrt).then_inc(s_std, 1)

            @block.sync
            def _(sp):
                if table is not None:
                    sp.wait_ge(s_y, NT)
                    sp.dma_start(table.rearrange("(t p) c -> p t c", p=P), y[:]).then_inc(s_out, 16)
                    sp.wait_ge(s_out, 16)


def project(nc, tag, cst, w, width, prep, preps, evac, evacs):
    with ExitStack() as ctx:
        a = Pool_(nc, ctx, tag)
        xs, xt = a.sb("xs", [P, TB, C]), a.sb("xt", [P, TB, C])
        turned, product = a.ps("turned", [P, TB + 1, C]), a.ps("product", [P, TB + 1, C])
        s_chain, s_xs, s_turned = a.sem("chain"), a.sem("xs"), a.sem("turned")
        s_xt, s_product = a.sem("xt"), a.sem("product")
        per = preps + evacs
        with nc.Block() as block:

            @block.vector
            def _(dve):
                link = Chain(dve, s_chain)
                with dve.Fori(0, TURNS) as i:
                    link.turn(i, per + 1)
                    prep(link, i, xs)
                    link(nc.vector.tensor_copy(xs[:, 0, 0:1], xs[:, 0, 0:1]))
                    dve.sem_inc(s_xs, 1)
                    dve.wait_ge(s_product, i + 1)
                    evac(link, i, product)
                link.end(TURNS)

            @block.tensor
            def _(pe):
                with pe.Fori(0, TURNS) as i:
                    pe.wait_ge(s_xs, i + 1)
                    for b in range(TB):
                        for k in range(KC):
                            last = nc.tensor.transpose(turned[:, b, k * P:(k + 1) * P],
                                                       xs[:, b, k * P:(k + 1) * P], cst["ident"][:])
                    last.then_inc(s_turned, 1)
                    pe.wait_ge(s_xt, i + 1)
                    for b in range(TB):
                        for k in range(KC):
                            last = nc.tensor.matmul(product[:, b, 0:width], xt[:, b, k * P:(k + 1) * P],
                                                    w[:, k, 0:width], start=(k == 0), stop=(k == KC - 1))
                    last.then_inc(s_product, 1)

            @block.scalar
            def _(act):
                with act.Fori(0, TURNS) as i:
                    act.wait_ge(s_turned, i + 1)
                    nc.scalar.copy(xt[:], turned[:, 0:TB, :]).then_inc(s_xt, 1)


def gather_sum(nc, cst, sorted0, gb, table, agg):
    with ExitStack() as ctx:
        a = Pool_(nc, ctx, "gsum")
        ix = [a.sb(f"ix{s}", [P, G], I32) for s in range(2)]
        rc = [a.sb(f"rc{s}", [P, G, 4]) for s in range(2)]
        hot = [a.sb(f"hot{s}", [P, G, P]) for s in range(2)]
        rows = [a.sb(f"rows{s}", [P, G, C]) for s in range(2)]
        part = [a.ps(f"part{s}", [P, 512]) for s in range(2)]
        s_chain, s_ix, s_hot, s_mm, s_go = (a.sem(n) for n in ("chain", "ix", "hot", "mm", "go"))
        s_rows = [a.sem(f"rows{s}") for s in range(2)]

        def groups(eng, step):
            step(0, 0)
            with eng.Fori(0, (NG - 2) // 2) as i:
                step(i * 2 + 1, 1)
                step(i * 2 + 2, 0)
            step(NG - 1, (NG - 1) % 2, last=True)

        with nc.Block() as block:

            @block.vector
            def _(dve):
                link, V = Chain(dve, s_chain), nc.vector
                link(V.memset(agg[:], 0.0))

                def prepare(g, s):
                    r = sorted0[:, bass.ds(g, 1), :].rearrange("p a (q r) -> p (a q) r", r=4)
                    V.tensor_copy(ix[s][:], r[:, :, 0]).then_inc(s_ix, 1)
                    link(V.tensor_copy(rc[s][:], r))
                    for q in range(G):
                        last = V.tensor_scalar(hot[s][:, q, :], cst["iota"][:], rc[s][:, q, 1:2],
                                               rc[s][:, q, 2:3], ALU.is_equal, ALU.mult)
                    last.then_inc(s_hot, 1)

                def take(g, s):
                    b = dve.value_load(gb[0:1, bass.ds(g, 1)], min_val=0, max_val=NT - 1)
                    dve.wait_ge(s_mm, g + 1)
                    to = agg[:, bass.ds(b, 1), :].rearrange("p a c -> p (a c)")
                    link(V.tensor_tensor(to, to, part[s][:, 0:C], ALU.add))

                def step(g, s, last=False):
                    if not isinstance(g, int):
                        link.turn(g - 1, 2)
                    if not last:
                        prepare(g + 1, 1 - s)
                    take(g, s)

                prepare(0, 0)
                step(0, 0)
                with dve.Fori(0, (NG - 2) // 2) as i:
                    link.turn(i, 4)
                    for g, s in ((i * 2 + 1, 1), (i * 2 + 2, 0)):
                        prepare(g + 1, 1 - s)
                        take(g, s)
                link.end((NG - 2) // 2)
                take(NG - 1, (NG - 1) % 2)

            @block.gpsimd
            def _(pool):
                def step(g, s, last=False):
                    pool.wait_ge(s_ix, g + 1)
                    pool.sem_inc(s_go, 1)
                    if not (isinstance(g, int) and g < 2):
                        pool.wait_ge(s_mm, g - 1)
                        pool.sem_inc(s_go, 1)
                    for q in range(G):
                        nc.gpsimd.indirect_dma_start(
                            rows[s][:, q, :], None, table,
                            bass.IndirectOffsetOnAxis(ap=ix[s][:, q:q + 1], axis=0)).then_inc(s_rows[s], 16)

                step(0, 0)
                step(1, 1)
                with pool.Fori(0, (NG - 2) // 2) as i:
                    step(i * 2 + 2, 0)
                    step(i * 2 + 3, 1)

            @block.tensor
            def _(pe):
                with pe.Fori(0, NG // 2) as i:
                    for s in range(2):
                        pe.wait_ge(s_hot, i * 2 + s + 1)
                        pe.wait_ge(s_rows[s], (i + 1) * (16 * G))
                        for q in range(G):
                            last = nc.tensor.matmul(part[s][:, 0:C], hot[s][:, q, :], rows[s][:, q, :],
                                                    start=(q == 0), stop=(q == G - 1))
                        last.then_inc(s_mm, 1)


def row_broadcast(sp, to, vec, sem):
    sp.dma_start(to, vec.unsqueeze(0).broadcast_to([P] + list(vec.shape))).then_inc(sem, 16)


def gnn0(nc, cst, A, x, n, agg):
    with ExitStack() as ctx:
        a = Pool_(nc, ctx, "gnn0")
        w, dg, bi = a.sb("w", [P, KC, C]), a.sb("dg", [P, C]), a.sb("bi", [P, C])
        s_in, s_dg = a.sem("in"), a.sem("dg")
        with nc.Block() as block:

            @block.sync
            def _(sp):
                row_broadcast(sp, dg[:], A["L0_gnn_learnable_diag"], s_in)
                row_broadcast(sp, bi[:], A["L0_gnn_bias"], s_in)
                sp.dma_start(w[:], A["L0_gnn_weight"].rearrange("(k p) c -> p k c", p=P)).then_inc(s_in, 16)

            @block.vector
            def _(dve):
                dve.wait_ge(s_in, 48)
                nc.vector.tensor_scalar(dg[:], dg[:], 1.0, None, ALU.add).then_inc(s_dg, 1)

        V = nc.vector

        def prep(link, i, xs):
            at = bass.ds(i * TB, TB)
            link(V.tensor_tensor(xs[:], agg[:, at, :], bc(dg[:], 1, TB), ALU.mult))
            link(V.tensor_tensor(xs[:], n[:, at, :], xs[:], ALU.subtract))

        def evac(link, i, ps):
            to = x[:, bass.ds(i * TB, TB), :]
            link(V.tensor_tensor(to, to, ps[:, 0:TB, :], ALU.add))
            link(V.tensor_tensor(to, to, bc(bi[:], 1, TB), ALU.add))

        project(nc, "gnn0p", cst, w, C, prep, 2, evac, 2)

def gate(nc, tag, cst, logits, K, keys, weights):
    ranks = len(weights)
    with ExitStack() as ctx:
        a = Pool_(nc, ctx, tag)
        top = [a.sb(f"top{r}", [P, NT]) for r in range(ranks)]
        eq, rev = a.sb("eq", [P, NT, K]), a.sb("rev", [P, K])
        s_chain, s_arg, s_exp = a.sem("chain"), a.sem("arg"), a.sem("exp")
        with nc.Block() as block:

            @block.vector
            def _(dve):
                link, V = Chain(dve, s_chain), nc.vector
                link(V.tensor_scalar(rev[:], cst["iota"][:, 0:K], -1.0, float(K), ALU.mult, ALU.add))
                for r in range(ranks):
                    key = keys[:, r * NT:(r + 1) * NT]
                    link(V.tensor_reduce(top[r][:], logits[:], AX, ALU.max))
                    link(V.tensor_tensor(eq[:], logits[:], bc(top[r][:], 2, K), ALU.is_equal))
                    link(V.tensor_tensor(eq[:], eq[:], bc(rev[:], 1, NT), ALU.mult))
                    link(V.tensor_reduce(key, eq[:], AX, ALU.max))
                    link(V.tensor_scalar(key, key, -1.0, float(K), ALU.mult, ALU.add))
                    if r < ranks - 1:
                        link(V.tensor_tensor(eq[:], bc(cst["iota"][:, 0:K], 1, NT), bc(key, 2, K), ALU.is_equal))
                        link(V.scalar_tensor_tensor(logits[:], eq[:], -BIG, logits[:], ALU.mult, ALU.add))
                if ranks == 2:
                    V.tensor_tensor(top[1][:], top[1][:], top[0][:], ALU.subtract).then_inc(s_arg, 1)
                    dve.wait_ge(s_exp, 1)
                    link(V.tensor_scalar(weights[0], top[1][:], 1.0, None, ALU.add))
                    link(V.reciprocal(weights[0], weights[0]))
                    link(V.tensor_tensor(weights[1], top[1][:], weights[0], ALU.mult))
                else:
                    V.tensor_tensor(logits[:], logits[:], bc(top[0][:], 2, K), ALU.subtract).then_inc(s_arg, 1)
                    dve.wait_ge(s_exp, 1)
                    link(V.tensor_reduce(weights[0], logits[:], AX, ALU.add))
                    link(V.reciprocal(weights[0], weights[0]))

            @block.scalar
            def _(act):
                act.wait_ge(s_arg, 1)
                to = top[1] if ranks == 2 else logits
                nc.scalar.activation(to[:], to[:], ACT.Exp).then_inc(s_exp, 1)


def route(nc, tag, cst, keys, ranks, K, tiles, B, pos, experts, tokens, table):
    J = ranks * NT
    with ExitStack() as ctx:
        a = Pool_(nc, ctx, tag)
        ids, fill = a.sb("ids", [P, J, 1]), a.sb("fill", [P, tiles])
        sort_positions(nc, tag + "s", cst, keys[:], P, J, K, P, pos[:], tiles, experts[:])
        s_ids, s_chain = a.sem("ids"), a.sem("chain")
        with nc.Block() as block:

            @block.gpsimd
            def _(pool):
                for r in range(ranks):
                    nc.gpsimd.iota(ids[:, r * NT:(r + 1) * NT, 0], pattern=[[P, NT]], base=0, channel_multiplier=1,
                                   allow_small_or_imprecise_dtypes=True).then_inc(s_ids, 1)
                nc.gpsimd.memset(fill[:], 0.0).then_inc(s_ids, 1)
                pool.wait_ge(s_ids, ranks + 1)

        scatter_rows(nc, tag + "w", pos[:], ids[:], table, P, J // (ranks * B), B,
                     (table.rearrange("(p t) r -> p (t r)", p=P), fill[:]), slots=ranks)
        by_tile, turned = a.sb("by_tile", [tiles, P]), a.ps("turned", [P, 512])
        s_in, s_turned = a.sem("in"), a.sem("turned")
        with nc.Block() as block:

            @block.sync
            def _(sp):
                sp.dma_start(by_tile[:], table.rearrange("(t p) r -> t (p r)", p=P)).then_inc(s_in, 16)

            @block.tensor
            def _(pe):
                pe.wait_ge(s_in, 16)
                nc.tensor.transpose(turned[:, 0:tiles], by_tile[:], cst["ident"][0:tiles, 0:tiles]).then_inc(s_turned, 1)

            @block.vector
            def _(dve):
                dve.wait_ge(s_turned, 1)
                nc.vector.tensor_copy(tokens[:], turned[:, 0:tiles]).then_inc(s_chain, 1)


def run_experts(nc, tag, cst, tiles, experts, tokens, rows_table, w1, w1_fixed, b1t, b1_fixed, FC, w2, b2, func, ytable):
    F = FC * P
    HB = (F + 511) // 512
    with ExitStack() as ctx:
        a = Pool_(nc, ctx, tag)
        two = range(2)
        ix = [a.sb(f"ix{s}", [P, 1], I32) for s in two]
        rows = [a.sb(f"rows{s}", [P, C]) for s in two]
        xt = [a.sb(f"xt{s}", [P, C]) for s in two]
        w1s = [a.sb(f"w1s{s}", [P, KC, F]) for s in two] if w1_fixed is None else [w1_fixed] * 2
        w2s = [a.sb(f"w2s{s}", [P, FC, C]) for s in two]
        ht = [a.sb(f"ht{s}", [P, FC, P]) for s in two]
        ys = [a.sb(f"ys{s}", [P, C]) for s in two]
        turned = a.ps("turned", [P, 512])
        hidden = [a.ps(f"hidden{s}", [P, HB * 512]) for s in two]
        y = [a.ps(f"y{s}", [P, 512]) for s in two]
        s_ix, s_turned, s_xt, s_hidden, s_ht, s_y, s_ys = (
            a.sem(m) for m in ("ix", "turned", "xt", "hidden", "ht", "y", "ys"))
        s_rows, s_w, s_out = ([a.sem(f"{m}{s}") for s in two] for m in ("rows", "w", "out"))
        s_go = a.sem("go")
        loads = 32 if w1_fixed is None else 16

        def tiles_by_two(eng, step):
            step(0, 0)
            step(1, 1)
            with eng.Fori(1, tiles // 2) as i:
                step(i * 2, 0)
                step(i * 2 + 1, 1)
            if tiles % 2:
                step(tiles - 1, 0)

        def early(t):
            return isinstance(t, int) and t < 2

        with nc.Block() as block:

            @block.sync
            def _(sp):
                def load(t, s):
                    e = sp.value_load(experts[0:1, bass.ds(t, 1)], min_val=0, max_val=w2.shape[0] - 1)
                    if not early(t):
                        sp.wait_ge(s_y, t - 1)
                    if w1_fixed is None:
                        sp.dma_start(w1s[s][:], w1[bass.ds(e, 1)].rearrange("a (k p) f -> p (a k) f", p=P)).then_inc(s_w[s], 16)
                    sp.dma_start(w2s[s][:], w2[bass.ds(e, 1)].rearrange("a (k p) c -> p (a k) c", p=P)).then_inc(s_w[s], 16)

                tiles_by_two(sp, load)

            @block.gpsimd
            def _(pool):
                def gather(t, s):
                    pool.wait_ge(s_ix, t + 1)
                    pool.sem_inc(s_go, 1)
                    if not early(t):
                        pool.wait_ge(s_turned, t - 1)
                        pool.sem_inc(s_go, 1)
                    nc.gpsimd.indirect_dma_start(
                        rows[s][:], None, rows_table,
                        bass.IndirectOffsetOnAxis(ap=ix[s][:, 0:1], axis=0)).then_inc(s_rows[s], 16)

                tiles_by_two(pool, gather)

            @block.vector
            def _(dve):
                V = nc.vector

                def index(t, s):
                    V.tensor_copy(ix[s][:], tokens[:, bass.ds(t, 1)]).then_inc(s_ix, 1)

                def take(t, s, after=None):
                    e = dve.value_load(experts[0:1, bass.ds(t, 1)], min_val=0, max_val=w2.shape[0] - 1)
                    dve.wait_ge(s_y, t + 1)
                    if not early(t):
                        n = t // 2 * 16 if isinstance(t, int) else (after * 16)
                        dve.wait_ge(s_out[s], n)
                    V.tensor_tensor(ys[s][:], y[s][:, 0:C], b2[:, bass.ds(e, 1), :].rearrange("p a c -> p (a c)"),
                                    ALU.add).then_inc(s_ys, 1)

                index(0, 0)
                index(1, 1)
                take(0, 0)
                index(2, 0)
                take(1, 1)
                index(3, 1)
                with dve.Fori(1, tiles // 2 - 1) as i:
                    for s in two:
                        take(i * 2 + s, s, i)
                        index(i * 2 + s + 2, s)
                last = tiles // 2 * 2
                take(last - 2, 0)
                if tiles % 2:
                    index(tiles - 1, 0)
                take(last - 1, 1)
                if tiles % 2:
                    take(tiles - 1, 0)

            @block.tensor
            def _(pe):
                def turn(s, n):
                    pe.wait_ge(s_rows[s], n)
                    for k in range(KC):
                        last = nc.tensor.transpose(turned[:, k * P:(k + 1) * P], rows[s][:, k * P:(k + 1) * P],
                                                   cst["ident"][:])
                    last.then_inc(s_turned, 1)

                def products(t, s, n, more=True):
                    pe.wait_ge(s_xt, t + 1)
                    pe.wait_ge(s_w[s], n * loads)
                    for f in range(FC):
                        for k in range(KC):
                            last = nc.tensor.matmul(hidden[s][:, f * P:(f + 1) * P], w1s[s][:, k, f * P:(f + 1) * P],
                                                    xt[s][:, k * P:(k + 1) * P], start=(k == 0), stop=(k == KC - 1))
                    last.then_inc(s_hidden, 1)
                    if more:
                        turn(1 - s, (n + s) * 16)
                    pe.wait_ge(s_ht, t + 1)
                    if not early(t):
                        pe.wait_ge(s_ys, t - 1)
                    for f in range(FC):
                        last = nc.tensor.matmul(y[s][:, 0:C], ht[s][:, f, :], w2s[s][:, f, :],
                                                start=(f == 0), stop=(f == FC - 1))
                    last.then_inc(s_y, 1)

                turn(0, 16)
                products(0, 0, 1)
                products(1, 1, 1)
                with pe.Fori(1, tiles // 2 - 1) as i:
                    products(i * 2, 0, i + 1)
                    products(i * 2 + 1, 1, i + 1)
                h = tiles // 2
                products(h * 2 - 2, 0, h)
                products(h * 2 - 1, 1, h, more=tiles % 2 == 1)
                if tiles % 2:
                    products(tiles - 1, 0, h + 1, more=False)

            @block.scalar
            def _(act):
                def step(t, s):
                    e = 0 if b1_fixed else act.value_load(experts[0:1, bass.ds(t, 1)], min_val=0, max_val=w2.shape[0] - 1)
                    act.wait_ge(s_turned, t + 1)
                    nc.scalar.copy(xt[s][:], turned[:, 0:C]).then_inc(s_xt, 1)
                    act.wait_ge(s_hidden, t + 1)
                    for f in range(FC):
                        bias = b1t[:, 0, f:f + 1] if b1_fixed else b1t[:, bass.ds(e, 1), f:f + 1].rearrange("p a b -> p (a b)")
                        last = nc.scalar.activation(ht[s][:, f, :], hidden[s][:, f * P:(f + 1) * P], func, bias=bias)
                    last.then_inc(s_ht, 1)
                    if not (isinstance(t, int) and t == 0):
                        store(t - 1, 1 - s)

                def store(t, s):
                    act.wait_ge(s_ys, t + 1)
                    nc.scalar.dma_start(ytable[bass.ds(t * P, P), :], ys[s][:]).then_inc(s_out[s], 16)

                tiles_by_two(act, step)
                store(tiles - 1, (tiles - 1) % 2)
                act.wait_ge(s_out[0], (tiles + 1) // 2 * 16)
                act.wait_ge(s_out[1], tiles // 2 * 16)


def fetch(nc, a, pos, J, ytable, got):
    s_got = a.sem("got")
    with nc.Block() as block:

        @block.gpsimd
        def _(pool):
            for j in range(J):
                nc.gpsimd.indirect_dma_start(got[:, j, :], None, ytable,
                                             bass.IndirectOffsetOnAxis(ap=pos[:, j:j + 1], axis=0)).then_inc(s_got, 16)
            pool.wait_ge(s_got, 16 * J)


def load_biases(nc, a, cst, b1, b1t, b2, b2b):
    rows = b1.shape[0] * b1.shape[1] // P
    flat, turned = a.sb("flat", [rows, P]), a.ps("turned", [P, 512])
    s_in, s_turned, s_done = a.sem("in"), a.sem("turned"), a.sem("done")
    with nc.Block() as block:

        @block.sync
        def _(sp):
            sp.dma_start(flat[:], b1.rearrange("e (f p) -> (e f) p", p=P)).then_inc(s_in, 16)
            row_broadcast(sp, b2b[:], b2, s_done)
            sp.wait_ge(s_done, 16)

        @block.tensor
        def _(pe):
            pe.wait_ge(s_in, 16)
            nc.tensor.transpose(turned[:, 0:rows], flat[:], cst["ident"][0:rows, 0:rows]).then_inc(s_turned, 1)

        @block.scalar
        def _(act):
            act.wait_ge(s_turned, 1)
            nc.scalar.copy(b1t[:].rearrange("p e f -> p (e f)"), turned[:, 0:rows]).then_inc(s_turned, 1)


def ffn0(nc, cst, A, x, n, ntab):
    ytab = nc.dram_tensor("ytab0", (S0 * P, C), F32, kind="Internal").ap()
    rtab = nc.dram_tensor("rtab0", (S0 * P, 1), F32, kind="Internal").ap()
    J = 2 * NT
    with ExitStack() as ctx:
        a = Pool_(nc, ctx, "ffn0")
        wt = [a.sb(f"wt{r}", [P, NT]) for r in range(2)]
        pos = a.sb("pos", [P, J], I32)
        with ExitStack() as c1:
            b = Pool_(nc, c1, "ffn0g")
            wg, bg = b.sb("wg", [P, KC, E0]), b.sb("bg", [P, E0])
            logits, keys = b.sb("logits", [P, NT, E0]), b.sb("keys", [P, J])
            experts, tokens = b.sb("experts", [1, S0], I32), b.sb("tokens", [P, S0], I32)
            b1t, b2b = b.sb("b1t", [P, E0, FC0]), b.sb("b2b", [P, E0, C])
            s_in = b.sem("in")
            with nc.Block() as block:

                @block.sync
                def _(sp):
                    sp.dma_start(wg[:], A["L0_ffn_gate_w"].rearrange("(k p) e -> p k e", p=P)).then_inc(s_in, 16)
                    row_broadcast(sp, bg[:], A["L0_ffn_gate_b"], s_in)
                    sp.wait_ge(s_in, 32)

            V = nc.vector

            def prep(link, i, xs):
                link(V.tensor_copy(xs[:], n[:, bass.ds(i * TB, TB), :]))

            def evac(link, i, ps):
                link(V.tensor_tensor(logits[:, bass.ds(i * TB, TB), :], ps[:, 0:TB, 0:E0], bc(bg[:], 1, TB), ALU.add))

            project(nc, "gate0p", cst, wg, E0, prep, 1, evac, 1)
            gate(nc, "gate0", cst, logits, E0, keys, [w[:] for w in wt])
            route(nc, "route0", cst, keys, 2, E0, S0, 5, pos, experts, tokens, rtab)
            with ExitStack() as c2:
                load_biases(nc, Pool_(nc, c2, "bias0"), cst, A["L0_ffn_b1"], b1t, A["L0_ffn_b2"], b2b)
            run_experts(nc, "exp0", cst, S0, experts, tokens, ntab, A["L0_ffn_w1"], None, b1t, False, FC0,
                        A["L0_ffn_w2"], b2b, ACT.Relu, ytab)
        with ExitStack() as c1:
            b = Pool_(nc, c1, "ffn0c")
            got = b.sb("got", [P, J, C])
            fetch(nc, b, pos, J, ytab, got)
            gb2 = b.sb("gb2", [P, 2, C])
            s_in, s_chain = b.sem("in"), b.sem("chain")
            with nc.Block() as block:

                @block.vector
                def _(dve):
                    link, V = Chain(dve, s_chain), nc.vector
                    for r in range(2):
                        part = got[:, r * NT:(r + 1) * NT, :]
                        link(V.tensor_tensor(part, part, bc(wt[r][:], 2, C), ALU.mult))
                    link(V.tensor_tensor(got[:, 0:NT, :], got[:, 0:NT, :], got[:, NT:J, :], ALU.add))
                    link(V.tensor_tensor(n[:], n[:], got[:, 0:NT, :], ALU.add))

            layernorm(nc, "lnm", n, got[:, 0:NT, :])
            with nc.Block() as block:

                @block.sync
                def _(sp):
                    row_broadcast(sp, gb2[:, 0, :], A["L0_ffn_gamma"], s_in)
                    row_broadcast(sp, gb2[:, 1, :], A["L0_ffn_beta"], s_in)

                @block.vector
                def _(dve):
                    link, V = Chain(dve, s_chain), nc.vector
                    link.n = 4
                    dve.wait_ge(s_in, 32)
                    y = got[:, 0:NT, :]
                    link(V.tensor_tensor(y, y, bc(gb2[:, 0, :], 1, NT), ALU.mult))
                    link(V.tensor_tensor(y, y, bc(gb2[:, 1, :], 1, NT), ALU.add))
                    link(V.tensor_tensor(x[:], x[:], y, ALU.add))


def ffn1(nc, cst, A, x, n, ntab):
    ytab = nc.dram_tensor("ytab1", (S1 * P, C), F32, kind="Internal").ap()
    rtab = nc.dram_tensor("rtab1", (S1 * P, 1), F32, kind="Internal").ap()
    with ExitStack() as ctx:
        a = Pool_(nc, ctx, "ffn1")
        wt, pos = a.sb("wt", [P, NT]), a.sb("pos", [P, NT], I32)
        with ExitStack() as c1:
            b = Pool_(nc, c1, "ffn1g")
            w1, wg, bg = b.sb("w1", [P, KC, F1]), b.sb("wg", [P, FC1, E1]), b.sb("bg", [P, E1])
            logits, keys = b.sb("logits", [P, NT, E1]), b.sb("keys", [P, NT])
            experts, tokens = b.sb("experts", [1, S1], I32), b.sb("tokens", [P, S1], I32)
            b1t, b2b = b.sb("b1t", [P, 1, FC1]), b.sb("b2b", [P, E1, C])
            with ExitStack() as c2:
                load_biases(nc, Pool_(nc, c2, "bias1"), cst, A["L1_ffn_b1"].unsqueeze(0), b1t, A["L1_ffn_bd"], b2b)
            with ExitStack() as c2:
                gate_hidden(nc, Pool_(nc, c2, "hid1"), cst, A, n, w1, wg, bg, b1t, logits)
            gate(nc, "gate1", cst, logits, E1, keys, [wt[:]])
            route(nc, "route1", cst, keys, 1, E1, S1, 5, pos, experts, tokens, rtab)
            run_experts(nc, "exp1", cst, S1, experts, tokens, ntab, None, w1, b1t, True, FC1,
                        A["L1_ffn_Wd"], b2b, ACT.Gelu, ytab)
        with ExitStack() as c1:
            b = Pool_(nc, c1, "ffn1c")
            got = b.sb("got", [P, NT, C])
            fetch(nc, b, pos, NT, ytab, got)
            s_chain = b.sem("chain")
            with nc.Block() as block:

                @block.vector
                def _(dve):
                    link, V = Chain(dve, s_chain), nc.vector
                    link(V.tensor_tensor(got[:], got[:], bc(wt[:], 2, C), ALU.mult))
                    link(V.tensor_tensor(x[:], x[:], got[:], ALU.add))


def gate_hidden(nc, a, cst, A, n, w1, wg, bg, b1t, logits):
    TN = TB * P // 2
    xs, xt = a.sb("xs", [P, TB, C]), a.sb("xt", [P, KC, TB * P])
    ht = a.sb("ht", [P, FC1, 2, TN])
    turned = a.ps("turned", [P, TB + 1, C])
    hidden = a.ps("hidden", [P, 4, 512])
    out = a.ps("out", [P, 512])
    s_in, s_xs, s_turned, s_xt, s_hidden, s_ht, s_out, s_took = (
        a.sem(m) for m in ("in", "xs", "turned", "xt", "hidden", "ht", "out", "took"))
    with nc.Block() as block:

        @block.sync
        def _(sp):
            sp.dma_start(w1[:], A["L1_ffn_W1"].rearrange("(k p) f -> p k f", p=P)).then_inc(s_in, 16)
            sp.dma_start(wg[:], A["L1_ffn_Wg"].rearrange("(k p) e -> p k e", p=P)).then_inc(s_in, 16)
            row_broadcast(sp, bg[:], A["L1_ffn_bg"], s_in)

        @block.vector
        def _(dve):
            V = nc.vector
            dve.wait_ge(s_in, 48)
            V.tensor_copy(xs[:], n[:, 0:TB, :]).then_inc(s_xs, 1)
            with dve.Fori(0, TURNS - 1) as i:
                dve.wait_ge(s_turned, i + 1)
                V.tensor_copy(xs[:], n[:, bass.ds((i + 1) * TB, TB), :]).then_inc(s_xs, 1)
                dve.wait_ge(s_out, i + 1)
                V.tensor_tensor(logits[:, bass.ds(i * TB, TB), :], out[:, 0:TB * E1].rearrange("p (t e) -> p t e", e=E1),
                                bc(bg[:], 1, TB), ALU.add).then_inc(s_took, 1)
            dve.wait_ge(s_out, TURNS)
            V.tensor_tensor(logits[:, NT - TB:NT, :], out[:, 0:TB * E1].rearrange("p (t e) -> p t e", e=E1),
                            bc(bg[:], 1, TB), ALU.add).then_inc(s_took, 1)

        @block.tensor
        def _(pe):
            pe.wait_ge(s_in, 48)

            def turn(i, first=False):
                pe.wait_ge(s_xs, i + 1)
                for b in range(TB):
                    for k in range(KC):
                        last = nc.tensor.transpose(turned[:, b, k * P:(k + 1) * P], xs[:, b, k * P:(k + 1) * P],
                                                   cst["ident"][:])
                last.then_inc(s_turned, 1)
                pe.wait_ge(s_xt, i + 1)
                for f in range(FC1):
                    if not (first and f < 2):
                        pe.wait_ge(s_ht, i * FC1 + f - 1)
                    for m in range(2):
                        for k in range(KC):
                            last = nc.tensor.matmul(hidden[:, f % 2 * 2 + m, 0:TN], w1[:, k, f * P:(f + 1) * P],
                                                    xt[:, k, m * TN:(m + 1) * TN], start=(k == 0), stop=(k == KC - 1))
                    last.then_inc(s_hidden, 1)
                pe.wait_ge(s_ht, (i + 1) * FC1)
                if not first:
                    pe.wait_ge(s_took, i)
                for b in range(TB):
                    for f in range(FC1):
                        last = nc.tensor.matmul(out[:, b * E1:(b + 1) * E1],
                                                ht[:, f].rearrange("p m n -> p (m n)")[:, b * P:(b + 1) * P],
                                                wg[:, f, :], start=(f == 0), stop=(f == FC1 - 1))
                last.then_inc(s_out, 1)

            turn(0, first=True)
            with pe.Fori(1, TURNS) as i:
                turn(i)

        @block.scalar
        def _(act):
            def turn(i, first=False):
                act.wait_ge(s_turned, i + 1)
                nc.scalar.copy(xt[:].rearrange("p k (b n) -> p b k n", b=TB),
                               turned[:, 0:TB, :].rearrange("p b (k n) -> p b k n", k=KC)).then_inc(s_xt, 1)
                if not first:
                    act.wait_ge(s_out, i)
                for f in range(FC1):
                    act.wait_ge(s_hidden, i * FC1 + f + 1)
                    nc.scalar.activation(ht[:, f], hidden[:, f % 2 * 2:f % 2 * 2 + 2, 0:TN], ACT.Gelu,
                                         bias=b1t[:, 0, f:f + 1]).then_inc(s_ht, 1)

            turn(0, first=True)
            with act.Fori(1, TURNS) as i:
                turn(i)


def split(link, V, parts, rest, src):
    link(V.tensor_copy(parts[0], src))
    link(V.tensor_tensor(rest, src, parts[0], ALU.subtract))
    link(V.tensor_copy(parts[1], rest))
    link(V.tensor_tensor(rest, rest, parts[1], ALU.subtract))
    link(V.tensor_copy(parts[2], rest))


def heads_table(nc, cst, A, n, hparts, hdram):
    with ExitStack() as ctx:
        a = Pool_(nc, ctx, "heads")
        htab = a.sb("htab", [P, NT, HR + H])
        rest = a.sb("rest", [P, TB, HN])
        wn, wt = a.sb("wn", [P, KC, C]), a.sb("wt", [P, KC, C])
        av, tmp = a.sb("av", [P, 2, C]), a.sb("tmp", [P, TB, C])
        turned = a.ps("turned", [P, KC, C])
        s_in, s_turned, s_wt, s_chain, s_out, s_split = (a.sem(m) for m in ("in", "turned", "wt", "chain", "out", "split"))
        with nc.Block() as block:

            @block.sync
            def _(sp):
                sp.dma_start(wn[:], A["L1_gnn_W"].rearrange("(o p) c -> p o c", p=P)).then_inc(s_in, 16)
                row_broadcast(sp, av[:, 0, :], A["L1_gnn_a_src"].rearrange("h d -> (h d)"), s_in)
                row_broadcast(sp, av[:, 1, :], A["L1_gnn_a_dst"].rearrange("h d -> (h d)"), s_in)
                sp.wait_ge(s_in, 48)

            @block.tensor
            def _(pe):
                pe.wait_ge(s_in, 48)
                for k in range(KC):
                    for o in range(KC):
                        last = nc.tensor.transpose(turned[:, k, o * P:(o + 1) * P], wn[:, o, k * P:(k + 1) * P],
                                                   cst["ident"][:])
                last.then_inc(s_turned, 1)

            @block.scalar
            def _(act):
                act.wait_ge(s_turned, 1)
                nc.scalar.copy(wt[:], turned[:]).then_inc(s_wt, 1)

            @block.vector
            def _(dve):
                nc.vector.memset(htab[:], 1.0).then_inc(s_chain, 1)

        V = nc.vector

        def prep(link, i, xs):
            link(V.tensor_copy(xs[:], n[:, bass.ds(i * TB, TB), :]))

        def evac(link, i, ps):
            at = bass.ds(i * TB, TB)
            row = htab[:, at, 0:HW].rearrange("p t (h d) -> p t h d", d=D + 1)[:, :, :, 0:D]
            link(V.tensor_copy(row, ps[:, 0:TB, :].rearrange("p t (h d) -> p t h d", d=D)))
            for k in range(2):
                link(V.tensor_tensor(tmp[:], ps[:, 0:TB, :], bc(av[:, k, :], 1, TB), ALU.mult))
                link(V.tensor_reduce(htab[:, at, HW + k * H:HW + (k + 1) * H],
                                     tmp[:].rearrange("p t (h d) -> p t h d", d=D), AX, ALU.add))

        project(nc, "headsp", cst, wt, C, prep, 1, evac, 5)
        with nc.Block() as block:

            @block.sync
            def _(sp):
                sp.dma_start(hdram.rearrange("(t p) c -> p t c", p=P), htab[:, :, 0:HR]).then_inc(s_out, 16)
                sp.wait_ge(s_out, 16)

            @block.vector
            def _(dve):
                link = Chain(dve, s_split)
                for t in range(0, NT, TB):
                    at = slice(t, t + TB)
                    split(link, V, [hparts[:, at, k, 0:C].rearrange("p t (h d) -> p t h d", d=D) for k in range(3)],
                          rest[:, :, 0:C].rearrange("p t (h d) -> p t h d", d=D),
                          htab[:, at, 0:HW].rearrange("p t (h d) -> p t h d", d=D + 1)[:, :, :, 0:D])
                    split(link, V, [hparts[:, at, k, C:HN] for k in range(3)], rest[:, :, C:HN], htab[:, at, HR:HR + H])


def edge_weights(nc, a, A, cst, sorted1, ewz, fields):
    wn = a.sb("wn", [P, KC, 3])
    turned = a.ps("turned", [P, 512])
    enc, encb, rest = a.sb("enc", [4, C]), a.sb("encb", [4, 3, C], BF16), a.sb("rest", [4, C])
    left = a.sb("left", [P, NG * G, 3])
    s_in, s_bias, s_turned, s_enc, s_zero, s_split, s_out, s_chain = (
        a.sem(m) for m in ("in", "bias", "turned", "enc", "zero", "split", "out", "chain"))
    with nc.Block() as block:

        @block.gpsimd
        def _(pool):
            nc.gpsimd.memset(ewz[:], 0.0).then_inc(s_zero, 1)

        @block.vector
        def _(dve):
            link, V = Chain(dve, s_chain), nc.vector
            rec = sorted1[:].rearrange("p g (q r) -> p (g q) r", r=8)
            split(link, V, [fields[:, :, 3 * j:3 * j + 3] for j in range(3)], left[:], rec[:, :, 2:5])
            link(V.tensor_copy(fields[:, :, PF - 1], rec[:, :, 5]))
            dve.wait_ge(s_bias, 16)
            dve.wait_ge(s_enc, 1)
            split(link, V, [encb[:, i, :] for i in range(3)], rest[:], enc[:])
            dve.sem_inc(s_split, 1)

        @block.sync
        def _(sp):
            sp.dma_start(wn[:], A["L1_gnn_edge_W"].rearrange("(o p) c -> p o c", p=P)).then_inc(s_in, 16)
            sp.dma_start(enc[3:4, :], A["L1_gnn_edge_b"].unsqueeze(0)).then_inc(s_bias, 16)
            sp.wait_ge(s_zero, 1)
            sp.wait_ge(s_split, 1)
            for q in range(G):
                for i in range(3):
                    at = q * 32 + i * PF
                    for j in range(3):
                        sp.dma_start(ewz[at + 3 * j:at + 3 * j + 3, q, :], encb[0:3, i, :]).then_inc(s_out, 16)
                    sp.dma_start(ewz[at + 9:at + 10, q, :], encb[3:4, i, :]).then_inc(s_out, 16)
            sp.wait_ge(s_out, 16 * 12 * G)

        @block.tensor
        def _(pe):
            pe.wait_ge(s_in, 16)
            for o in range(KC):
                last = nc.tensor.transpose(turned[0:3, o * P:(o + 1) * P], wn[:, o, :], cst["ident"][:])
            last.then_inc(s_turned, 1)

        @block.scalar
        def _(act):
            act.wait_ge(s_turned, 1)
            nc.scalar.copy(enc[0:3, :], turned[0:3, 0:C]).then_inc(s_enc, 1)


def attention(nc, cst, A, sorted1, gb, hparts, hdram, acc):
    with ExitStack() as ctx:
        a = Pool_(nc, ctx, "att")
        two, four = range(2), range(4)
        ewz = a.sb("ewz", [P, G, C], BF16)
        fields = a.sb("fields", [P, NG * G, PF], BF16)
        top = a.sb("top", [P, NT, H])
        with ExitStack() as c1:
            edge_weights(nc, Pool_(nc, c1, "ew"), A, cst, sorted1, ewz, fields)
        ix = [a.sb(f"ix{s}", [P, G], I32) for s in four]
        rc = [a.sb(f"rc{s}", [P, G * 8]) for s in four]
        hot = [a.sb(f"hot{s}", [P, G, P]) for s in four]
        hotb = [a.sb(f"hotb{s}", [P, G, P], BF16) for s in four]
        hott = [a.sb(f"hott{s}", [P, G, P], BF16) for s in four]
        rcb = [a.sb(f"rcb{s}", [P, G, 32], BF16) for s in four]
        rct = [a.sb(f"rct{s}", [P, P], BF16) for s in four]
        rows = [a.sb(f"rows{s}", [P, G, HR]) for s in four]
        enc = a.sb("enc", [P, G, C])
        al = [a.sb(f"al{s}", [P, G, H]) for s in two]
        alb = [a.sb(f"alb{s}", [P, 2, G * H], BF16) for s in four]
        line = a.sb("line", [G * H, 2, P])
        same, run = a.sb("same", [G * H, P + 1]), a.sb("run", [G * H, P])
        pen = a.sb("pen", [G * H, P])
        ends = a.sb("ends", [G * H, 2, P], BF16)
        back = a.sb("back", [P, 2, G * H], BF16)
        cand, gtop = a.sb("cand", [P, G, H]), a.sb("gtop", [P, H])
        ntop = a.sb("ntop", [P, H], BF16)
        fall = [a.sb(f"fall{s}", [P, H]) for s in two]
        dif = a.sb("dif", [P, G, H])
        ex = a.sb("ex", [P, G, H])
        msg = [a.sb(f"msg{s}", [P, G, HW]) for s in two]
        p_hot = a.ps("p_hot", [P, 2, G, P], BF16)
        p_h = a.ps("p_h", [P, G, C])
        p_z = a.ps("p_z", [P, G, C])
        p_small = a.ps("p_small", [P, 512])
        p_line = a.ps("p_line", [P, 1024], BF16)
        p_acc = a.ps("p_acc", [P, 512])
        a_adst = p_z[:, 0, 0:G * H]
        a_line = p_line[0:G * H, 0:2 * P]
        a_back = p_line[:, 512:512 + 2 * G * H]
        a_top = p_small[:, 192:192 + G * 2 * H]
        a_edge = p_small[:, 256:256 + G * H]
        sems = {m: a.sem(m) for m in ("chain", "ix", "hot", "p_hot", "hott", "hz", "al", "p_line", "line", "ends",
                                      "p_back", "back", "p_top", "ntop", "p_edge", "dif", "ex", "msg", "p_acc", "go",
                                      "fall", "took", "p_z", "enc", "go_pe", "hotb")}
        s_rows = [a.sem(f"rows{s}") for s in four]
        LOOPED = (NG - 5) // 4

        def ahead(eng, step):
            step(0, 0, 0)
            step(1, 1, 0)
            with eng.Fori(0, LOOPED) as i:
                for k in range(2, 6):
                    step(i * 4 + k, k, i)
            for g in range(4 * LOOPED + 2, NG):
                step(g, g % 4, g // 4)

        with nc.Block() as block:

            @block.gpsimd
            def _(pool):
                def gather(g, s):
                    pool.wait_ge(sems["ix"], g + 1)
                    pool.sem_inc(sems["go"], 1)
                    for q in range(G):
                        nc.gpsimd.indirect_dma_start(
                            rows[s][:, q, :], None, hdram,
                            bass.IndirectOffsetOnAxis(ap=ix[s][:, q:q + 1], axis=0)).then_inc(s_rows[s], 16)

                with pool.Fori(0, NG // 4) as i:
                    for s in four:
                        gather(i * 4 + s, s)
                for g in range(NG // 4 * 4, NG):
                    gather(g, g % 4)

            @block.vector
            def _(dve):
                link, V = Chain(dve, sems["chain"]), nc.vector

                def index(g, s):
                    r = sorted1[:, bass.ds(g, 1), :].rearrange("p a (q r) -> p (a q) r", r=8)
                    V.tensor_copy(ix[s][:], r[:, :, 0]).then_inc(sems["ix"], 1)

                def places(g, s):
                    link(V.tensor_copy(rc[s][:], sorted1[:, bass.ds(g, 1), :].rearrange("p a x -> p (a x)")))
                    r = rc[s][:].rearrange("p (q r) -> p q r", r=8)
                    V.tensor_copy(alb[s][:, 1, :].rearrange("p (q h) -> p q h", h=H), bc(r[:, :, 1], 2, H))
                    f = fields[:, bass.ds(g * G, G), :]
                    V.tensor_copy(rcb[s][:, :, 0:3 * PF].rearrange("p q (i f) -> p q i f", f=PF), bc(f, 2, 3))
                    for q in range(G):
                        last = V.tensor_scalar(hot[s][:, q, :], cst["iota"][:], rc[s][:, q * 8 + 1:q * 8 + 2],
                                               None, ALU.is_equal)
                    last.then_inc(sems["hot"], 1)

                def alphas(g, k, turn):
                    dve.wait_ge(sems["hz"], g + 1)
                    dve.wait_ge(sems["enc"], g + 1)
                    link(V.tensor_tensor(enc[:], enc[:], p_h[:], ALU.mult))
                    link(V.tensor_reduce(al[k % 2][:], enc[:].rearrange("p q (h d) -> p q h d", d=D), AX, ALU.add))
                    link(V.tensor_tensor(al[k % 2][:], al[k % 2][:], a_adst.rearrange("p (q h) -> p q h", h=H), ALU.add))
                    dve.wait_ge(s_rows[k % 4], turn * (16 * G))
                    link(V.tensor_tensor(al[k % 2][:], al[k % 2][:], rows[k % 4][:, :, HW:HR], ALU.add))
                    link(V.scalar_tensor_tensor(al[k % 2][:], al[k % 2][:], 0.2, al[k % 2][:], ALU.mult, ALU.max))
                    real = rc[k % 4][:].rearrange("p (q r) -> p q r", r=8)[:, :, 5]
                    link(V.tensor_tensor(al[k % 2][:], al[k % 2][:], bc(real, 2, H), ALU.mult))
                    V.tensor_copy(alb[k % 4][:, 0, :], al[k % 2][:].rearrange("p q h -> p (q h)")).then_inc(sems["al"], 1)

                def segments(g):
                    dve.wait_ge(sems["line"], g + 1)
                    link(V.tensor_tensor(same[:, 1:P], line[:, 1, 1:P], line[:, 1, 0:P - 1], ALU.is_equal))
                    link(V.tensor_scalar(pen[:], same[:, 0:P], -1.0, BIG, ALU.add, ALU.mult))
                    link(V.tensor_tensor_scan(run[:], pen[:], line[:, 0, :], 0.0, ALU.add, ALU.max))
                    link(V.tensor_scalar(ends[:, 1, :], same[:, 1:P + 1], -1.0, 1.0, ALU.mult, ALU.add))
                    V.tensor_tensor(ends[:, 0, :], run[:], ends[:, 1, :], ALU.mult).then_inc(sems["ends"], 1)

                def maxima(g, s):
                    b = dve.value_load(gb[0:1, bass.ds(g, 1)], min_val=0, max_val=NT - 1)
                    dve.wait_ge(sems["p_top"], g + 1)
                    t = a_top.rearrange("p (q k h) -> p q k h", q=G, k=2)
                    link(V.tensor_scalar(cand[:], t[:, :, 1, :], -1.0, BIG, ALU.add, ALU.mult))
                    link(V.tensor_tensor(cand[:], cand[:], t[:, :, 0, :], ALU.add))
                    link(V.tensor_reduce(gtop[:], cand[:].rearrange("p q h -> p h q"), AX, ALU.max))
                    old = top[:, bass.ds(b, 1), :].rearrange("p a h -> p (a h)")
                    link(V.tensor_tensor(ntop[:], gtop[:], old, ALU.max))
                    dve.sem_inc(sems["ntop"], 1)
                    link(V.tensor_tensor(fall[s][:], old, ntop[:], ALU.subtract))
                    dve.sem_inc(sems["fall"], 1)
                    link(V.tensor_copy(old, ntop[:]))

                def exponents(g, s):
                    dve.wait_ge(sems["p_edge"], g + 1)
                    V.tensor_tensor(dif[:], al[s][:], a_edge.rearrange("p (q h) -> p q h", h=H),
                                    ALU.subtract).then_inc(sems["dif"], 1)

                def messages(g, k):
                    dve.wait_ge(sems["ex"], g + 1)
                    V.tensor_tensor(msg[k % 2][:].rearrange("p q (h d) -> p q h d", d=D + 1),
                                    rows[k % 4][:, :, 0:HW].rearrange("p q (h d) -> p q h d", d=D + 1),
                                    bc(ex[:], 3, D + 1), ALU.mult).then_inc(sems["msg"], 1)

                def gathered(g, s):
                    b = dve.value_load(gb[0:1, bass.ds(g, 1)], min_val=0, max_val=NT - 1)
                    to = acc[:, bass.ds(b, 1), :].rearrange("p a (h d) -> p (a h) d", d=D + 1)
                    link(V.tensor_tensor(to, to, bc(fall[s][:], 2, D + 1), ALU.mult))
                    dve.wait_ge(sems["p_acc"], g + 1)
                    link(V.tensor_tensor(to, to, p_acc[:, 0:HW].rearrange("p (h d) -> p h d", d=D + 1), ALU.add))
                    dve.sem_inc(sems["took"], 1)

                def step(g, k, i):
                    late = not isinstance(g, int)
                    if late and k == 2:
                        link.turn(i, 4 * (6 + 1 + 6 + 4 + 2))
                    maxima(g, k % 2)
                    if late or g + 3 < NG:
                        if late or g > 0:
                            dve.wait_ge(sems["msg"], g)
                        index(g + 3, (k + 3) % 4)
                    if late or g + 2 < NG:
                        places(g + 2, (k + 2) % 4)
                    if late or g + 1 < NG:
                        alphas(g + 1, k + 1, i + (k + 1) // 4 + 1)
                    exponents(g, k % 2)
                    if late or g + 1 < NG:
                        segments(g + 1)
                    messages(g, k)
                    if late or g > 0:
                        gathered(g - 1, (k + 1) % 2)
                    if late and k == 5:
                        link.end(LOOPED)

                link(V.memset(acc[:], 0.0))
                link(V.memset(top[:], -BIG))
                link(V.memset(same[:], 0.0))
                for s in four:
                    link(V.memset(rcb[s][:], 0.0))
                for g in range(3):
                    index(g, g)
                places(0, 0)
                places(1, 1)
                alphas(0, 0, 1)
                segments(0)
                ahead(dve, step)
                gathered(NG - 1, (NG - 1) % 2)

            @block.tensor
            def _(pe):
                T = nc.tensor

                def lines(g, s):
                    pe.wait_ge(sems["al"], g + 1)
                    pe.sem_inc(sems["go_pe"], 1)
                    T.transpose(a_line[:, 0:P], alb[s][:, 0, :], cst["identb"][:])
                    T.transpose(a_line[:, P:2 * P], alb[s][:, 1, :], cst["identb"][:]).then_inc(sems["p_line"], 1)

                def backs(g):
                    pe.wait_ge(sems["ends"], g + 1)
                    pe.sem_inc(sems["go_pe"], 1)
                    for k in range(2):
                        last = T.transpose(a_back[:, k * G * H:(k + 1) * G * H], ends[:, k, :],
                                           cst["identb"][0:G * H, 0:G * H])
                    last.then_inc(sems["p_back"], 1)

                def turn_places(g, s):
                    pe.wait_ge(sems["hotb"], g + 1)
                    T.transpose(p_hot[:, 1, 0, :], rcb[s][:].rearrange("p q f -> p (q f)"), cst["identb"][:])
                    for q in range(G):
                        last = T.transpose(p_hot[:, 0, q, :], hotb[s][:, q, :], cst["identb"][:])
                    last.then_inc(sems["p_hot"], 1)

                def tops(g, s):
                    pe.wait_ge(sems["back"], g + 1)
                    for q in range(G):
                        last = T.matmul(a_top[:, q * 2 * H:(q + 1) * 2 * H].rearrange("p (k h) -> p k h", k=2),
                                        hotb[s][:, q, :], back[:, :, q * H:(q + 1) * H], start=True, stop=True)
                    last.then_inc(sems["p_top"], 1)

                def destinations(g, s):
                    b = pe.value_load(gb[0:1, bass.ds(g, 1)], min_val=0, max_val=NT - 1)
                    pe.wait_ge(sems["hott"], g + 1)
                    node = hparts[:, bass.ds(b, 1), :, :].rearrange("p a k c -> p (a k) c")
                    for q in range(G):
                        last = T.matmul(p_z[:, q, :], rct[s][:], ewz[:, q, :], start=True, stop=True)
                    last.then_inc(sems["p_z"], 1)
                    for q in range(G):
                        for k in range(3):
                            T.matmul(p_h[:, q, :], hott[s][:, q, :], node[:, k, 0:C], start=(k == 0), stop=(k == 2))
                    pe.wait_ge(sems["enc"], g + 1)
                    for q in range(G):
                        for k in range(3):
                            last = T.matmul(a_adst[:, q * H:(q + 1) * H], hott[s][:, q, :], node[:, k, C:HN],
                                            start=(k == 0), stop=(k == 2))
                    last.then_inc(sems["hz"], 1)

                def edge_tops(g, s):
                    pe.wait_ge(sems["ntop"], g + 1)
                    for q in range(G):
                        last = T.matmul(a_edge[:, q * H:(q + 1) * H], hott[s][:, q, :], ntop[:], start=True, stop=True)
                    last.then_inc(sems["p_edge"], 1)

                def sums(g, k, first=False):
                    pe.wait_ge(sems["msg"], g + 1)
                    if not first:
                        pe.wait_ge(sems["took"], g)
                    for q in range(G):
                        last = T.matmul(p_acc[:, 0:HW], hot[k % 4][:, q, :], msg[k % 2][:, q, :], start=(q == 0), stop=(q == G - 1))
                    last.then_inc(sems["p_acc"], 1)

                def step(g, k, i):
                    late = not isinstance(g, int)
                    if late or g > 0:
                        sums(g - 1, k + 3, first=not late and g == 1)
                    edge_tops(g, k % 4)
                    if late or g + 2 < NG:
                        turn_places(g + 2, (k + 2) % 4)
                    if late or g + 1 < NG:
                        lines(g + 1, (k + 1) % 4)
                    if late or g + 2 < NG:
                        destinations(g + 2, (k + 2) % 4)
                    if late or g + 1 < NG:
                        backs(g + 1)
                        tops(g + 1, (k + 1) % 4)

                turn_places(0, 0)
                destinations(0, 0)
                turn_places(1, 1)
                lines(0, 0)
                destinations(1, 1)
                backs(0)
                tops(0, 0)
                ahead(pe, step)
                sums(NG - 1, NG - 1)

            @block.scalar
            def _(act):
                S = nc.scalar

                def copy_places(g, s):
                    act.wait_ge(sems["hot"], g + 1)
                    S.copy(hotb[s][:], hot[s][:]).then_inc(sems["hotb"], 1)
                    act.wait_ge(sems["p_hot"], g + 1)
                    S.copy(rct[s][:], p_hot[:, 1, 0, :])
                    S.copy(hott[s][:], p_hot[:, 0]).then_inc(sems["hott"], 1)

                def encodings(g):
                    act.wait_ge(sems["p_z"], g + 1)
                    S.activation(enc[:], p_z[:], ACT.Relu).then_inc(sems["enc"], 1)

                def copy_lines(g):
                    act.wait_ge(sems["p_line"], g + 1)
                    S.copy(line[:], a_line.rearrange("p (k n) -> p k n", k=2)).then_inc(sems["line"], 1)

                def copy_back(g):
                    act.wait_ge(sems["p_back"], g + 1)
                    S.copy(back[:], a_back.rearrange("p (k n) -> p k n", k=2)).then_inc(sems["back"], 1)

                def step(g, k, i):
                    late = not isinstance(g, int)
                    act.wait_ge(sems["fall"], g + 1)
                    S.activation(fall[k % 2][:], fall[k % 2][:], ACT.Exp)
                    if late or g + 2 < NG:
                        copy_places(g + 2, (k + 2) % 4)
                    if late or g + 1 < NG:
                        copy_lines(g + 1)
                    act.wait_ge(sems["dif"], g + 1)
                    S.activation(ex[:], dif[:], ACT.Exp).then_inc(sems["ex"], 1)
                    if late or g + 2 < NG:
                        encodings(g + 2)
                    if late or g + 1 < NG:
                        copy_back(g + 1)

                copy_places(0, 0)
                encodings(0)
                copy_places(1, 1)
                copy_lines(0)
                encodings(1)
                copy_back(0)
                ahead(act, step)


def gnn1(nc, cst, A, x, n, sorted1, gb):
    hdram = nc.dram_tensor("hdram", (NPAD, HR), F32, kind="Internal").ap()
    with ExitStack() as ctx:
        a = Pool_(nc, ctx, "gnn1")
        hparts, acc = a.sb("hparts", [P, NT, 3, HN], BF16), a.sb("acc", [P, NT, HW])
        heads_table(nc, cst, A, n, hparts, hdram)
        attention(nc, cst, A, sorted1, gb, hparts, hdram, acc)
        bi, den = a.sb("bi", [P, C]), a.sb("den", [P, NT, H])
        s_in, s_chain = a.sem("in"), a.sem("chain")
        with nc.Block() as block:

            @block.sync
            def _(sp):
                row_broadcast(sp, bi[:], A["L1_gnn_bias"], s_in)

            @block.vector
            def _(dve):
                link, V = Chain(dve, s_chain), nc.vector
                out = acc[:].rearrange("p t (h d) -> p t h d", d=D + 1)
                link(V.tensor_scalar(den[:], out[:, :, :, D], 1e-10, None, ALU.max))
                link(V.reciprocal(den[:], den[:]))
                for t in range(0, NT, TB):
                    part = out[:, t:t + TB, :, 0:D]
                    to = x[:, t:t + TB, :]
                    link(V.tensor_tensor(part, part, bc(den[:, t:t + TB, :], 3, D), ALU.mult))
                    link(V.tensor_tensor(to.rearrange("p t (h d) -> p t h d", d=D),
                                         to.rearrange("p t (h d) -> p t h d", d=D), part, ALU.add))
                dve.wait_ge(s_in, 16)
                link(V.tensor_tensor(x[:], x[:], bc(bi[:], 1, NT), ALU.add))


def build(nc, A, out, debug=None):
    spent.clear()
    with ExitStack() as ctx:
        top = Pool_(nc, ctx, "top")
        cst = {n: top.sb(n, [P, P]) for n in ("iota", "lower", "ident", "ones")}
        cst["identb"] = top.sb("identb", [P, P], BF16)
        with ExitStack() as c1:
            constants(nc, Pool_(nc, c1, "const"), cst)
        sorted0, sorted1 = top.sb("sorted0", [P, NG, G * 4]), top.sb("sorted1", [P, NG, G * 8])
        gb = [top.sb(f"gb{k}", [1, NG], I32) for k in range(2)]
        tab0 = nc.dram_tensor("tab0", (NG * GE, 4), F32, kind="Internal").ap()
        tab1 = nc.dram_tensor("tab1", (NG * GE, 8), F32, kind="Internal").ap()
        with ExitStack() as c1:
            a = Pool_(nc, c1, "edges")
            ek = [a.sb(f"key{k}", [P, EJ]) for k in range(2)]
            rec0, rec1 = a.sb("rec0", [P, EJ, 4]), a.sb("rec1", [P, EJ, 8])
            pos = [a.sb(f"pos{k}", [P, EJ], I32) for k in range(2)]
            fill, unsorted = a.sb("fill", [P, NG, G * 8]), a.sb("unsorted", [1, 1], I32)
            with ExitStack() as c2:
                edge_keys(nc, Pool_(nc, c2, "keys"), A, cst, ek, rec0, rec1, unsorted)
            padding(nc, fill)
            order_places(nc, cst, ek[1], rec1, pos[1], unsorted)
            for k in range(2):
                sort_positions(nc, f"sort{k}", cst, ek[k][:EP], EP, EJ, NT, GE, pos[k][:EP], NG, gb[k][:])
            f0 = fill[:].rearrange("p g x -> p (g x)")[:, 0:NG * G * 4]
            scatter_rows(nc, "scat0", pos[0][:EP], rec0[:EP], tab0, EP, 25, 8,
                         (tab0.rearrange("(p x) r -> p (x r)", p=P), f0))
            scatter_rows(nc, "scat1", pos[1][:EP], rec1[:EP], tab1, EP, 25, 8,
                         (tab1.rearrange("(p x) r -> p (x r)", p=P), fill[:].rearrange("p g x -> p (g x)")))
        with ExitStack() as c1:
            load_sorted(nc, Pool_(nc, c1, "back"), (tab0, tab1), (sorted0, sorted1))
        if debug == "sort":
            return
        x, n = top.sb("x", [P, NT, C]), top.sb("n", [P, NT, C])
        ntab = nc.dram_tensor("ntab", (NPAD, C), F32, kind="Internal").ap()
        with ExitStack() as c1:
            load_nodes(nc, Pool_(nc, c1, "load"), A["x"], x)
        layernorm(nc, "ln0", x, n, ntab)
        with ExitStack() as c1:
            agg = Pool_(nc, c1, "agg").sb("agg", [P, NT, C])
            gather_sum(nc, cst, sorted0, gb[0], ntab, agg)
            gnn0(nc, cst, A, x, n, agg)
        if debug == "gnn0":
            with ExitStack() as c1:
                store_nodes(nc, Pool_(nc, c1, "store"), x, out)
            return
        layernorm(nc, "ln1", x, n, ntab)
        ffn0(nc, cst, A, x, n, ntab)
        if debug == "ffn0":
            with ExitStack() as c1:
                store_nodes(nc, Pool_(nc, c1, "store"), x, out)
            return
        reuse_semaphores(nc)
        layernorm(nc, "ln2", x, n)
        gnn1(nc, cst, A, x, n, sorted1, gb[1])
        if debug == "gnn1":
            with ExitStack() as c1:
                store_nodes(nc, Pool_(nc, c1, "store"), x, out)
            return
        reuse_semaphores(nc)
        layernorm(nc, "ln3", x, n, ntab)
        ffn1(nc, cst, A, x, n, ntab)
        with ExitStack() as c1:
            store_nodes(nc, Pool_(nc, c1, "store"), x, out)



def padding(nc, fill):
    with nc.semaphore("pad_chain") as s_chain, nc.Block() as block:

        @block.vector
        def _(dve):
            link = Chain(dve, s_chain)
            link(nc.vector.memset(fill[:], 0.0))
            link(nc.vector.memset(fill[:].rearrange("p g (q r) -> p (g q) r", r=4)[:, :, 1], -1.0))


_INS = ['x', 'src', 'dst', 'edge_attr_3', 'edge_weight', 'L0_gnn_weight', 'L0_gnn_learnable_diag', 'L0_gnn_bias',
        'L0_ffn_gate_w', 'L0_ffn_gate_b', 'L0_ffn_w1', 'L0_ffn_b1', 'L0_ffn_w2', 'L0_ffn_b2', 'L0_ffn_gamma',
        'L0_ffn_beta', 'L1_gnn_W', 'L1_gnn_a_src', 'L1_gnn_a_dst', 'L1_gnn_edge_W', 'L1_gnn_edge_b', 'L1_gnn_bias',
        'L1_ffn_W1', 'L1_ffn_b1', 'L1_ffn_Wg', 'L1_ffn_bg', 'L1_ffn_Wd', 'L1_ffn_bd']
_OUT = ((N, C), 'float32')


def kernel(**inputs):
    import numpy as np
    import concourse.bacc as bacc
    from concourse.bass_utils import run_bass_kernel_spmd

    nc = bacc.Bacc("TRN2", target_bir_lowering=False, num_devices=1)
    arrays, args = {}, {}
    for name in _INS:
        a = np.ascontiguousarray(inputs[name])
        arrays[f"in_{name}"] = a
        args[name] = nc.dram_tensor(f"in_{name}", a.shape, mybir.dt.from_np(a.dtype), kind="ExternalInput").ap()
    out = nc.dram_tensor("out_dram", _OUT[0], F32, kind="ExternalOutput").ap()
    build(nc, args, out)
    r = run_bass_kernel_spmd(nc, [arrays], core_ids=[0])
    return r.results[0]["out_dram"]
```

```python
import concourse.bass as bass
from concourse import mybir
from concourse.alu_op_type import AluOpType as ALU
from contextlib import ExitStack, contextmanager

F32 = mybir.dt.float32
I32 = mybir.dt.int32
BF16 = mybir.dt.bfloat16
ACT = mybir.ActivationFunctionType
AX = mybir.AxisListType.X

P = 128
N = 3125
C = 256
KC = C // P
NT = (N + P - 1) // P
NPAD = NT * P
E = 50000
EP, EJ = 125, 400
G = 4
GE = G * P
NG = (E + NT * (GE - 1)) // GE
H, D = 8, 32
E0, F0 = 16, 512
E1, F1 = 8, 1024
FC0, FC1 = F0 // P, F1 // P
S0 = (2 * NPAD + E0 * (P - 1)) // P
S1 = (NPAD + E1 * (P - 1)) // P
EPS = 1e-5
BIG = 2.0 ** 100


class Chain:

    def __init__(self, eng, sem):
        self.eng, self.sem, self.base, self.n = eng, sem, 0, 0

    def __call__(self, ins):
        self.n += 1
        ins.then_inc(self.sem, 1)
        self.eng.wait_ge(self.sem, self.base + self.n)

    def turn(self, i, per):
        self.start, self.per = (self.base + self.n if not hasattr(self, "start") else self.start), per
        self.base, self.n = self.start + i * per, 0

    def end(self, turns):
        assert self.n == self.per, (self.n, self.per)
        self.base, self.n = self.start + turns * self.per, 0
        del self.start


class Pool_:

    def __init__(self, nc, ctx, tag):
        self.nc, self.ctx, self.tag = nc, ctx, tag

    def sb(self, name, shape, dt=F32):
        return self.ctx.enter_context(self.nc.sbuf_tensor(f"{self.tag}_{name}", shape, dt))

    def ps(self, name, shape, dt=F32):
        return self.ctx.enter_context(self.nc.psum_tensor(f"{self.tag}_{name}", shape, dt))

    def sem(self, name):
        sem = self.nc.alloc_semaphore(f"{self.tag}_{name}")
        self.ctx.callback(spent.append, sem)
        return sem


spent = []


def reuse_semaphores(nc):
    nc.clear_and_free_semaphores(list(spent))
    spent.clear()
    nc.all_engine_barrier()


def bc(ap, at, n):
    shape = list(ap.shape)
    ap = ap.unsqueeze(at)
    return ap.broadcast_to(shape[:at] + [n] + shape[at:])


@contextmanager
def guarded(eng, only_if):
    if only_if is None:
        yield
    else:
        flag = eng.value_load(only_if, min_val=0, max_val=P)
        with eng.If(flag > 0):
            yield


def sort_positions(nc, tag, cst, key, PK, J, K, unit, pos, ngroups, group_bucket, only_if=None):
    shift = unit.bit_length() - 1
    with ExitStack() as ctx:
        a = Pool_(nc, ctx, tag)
        mask = a.sb("mask", [P, K, J])
        seen = a.sb("seen", [P, K, J])
        before = a.sb("before", [P, K])
        count = a.sb("count", [P, K])
        ti = a.sb("ti", [P, K], I32)
        groups = a.sb("groups", [P, K])
        ends = a.sb("ends", [P, K])
        base = a.sb("base", [P, K])
        posf = a.sb("posf", [P, J])
        cmp = a.sb("cmp", [1, ngroups, K])
        gbf = a.sb("gbf", [1, ngroups])
        below_ps = a.ps("below", [P, 512])
        total_ps = a.ps("total", [P, 512])
        s_chain, s_count, s_sums = a.sem("chain"), a.sem("count"), a.sem("sums")
        with nc.Block() as block:

            @block.vector
            def _(dve):
                with guarded(dve, only_if):
                    link = Chain(dve, s_chain)
                    V = nc.vector
                    link(V.tensor_tensor(mask[:PK], bc(key, 1, K), bc(cst["iota"][:PK, 0:K], 2, J), ALU.is_equal))
                    flat = mask[:PK].rearrange("p k j -> p (k j)")
                    link(V.tensor_tensor_scan(seen[:PK].rearrange("p k j -> p (k j)"), flat, flat, 0.0, ALU.add, ALU.max))
                    link(V.memset(before[:PK, 0:1], 0.0))
                    link(V.tensor_copy(before[:PK, 1:K], seen[:PK, 0:K - 1, J - 1]))
                    V.tensor_tensor(count[:PK], seen[:PK, :, J - 1], before[:PK], ALU.subtract).then_inc(s_count, 1)
                    dve.wait_ge(s_sums, 1)
                    link(V.tensor_scalar(ti[:], total_ps[:, 0:K], float(unit - 1), None, ALU.add))
                    link(V.tensor_scalar(ti[:], ti[:], shift, None, ALU.arith_shift_right))
                    link(V.tensor_copy(groups[:], ti[:]))
                    link(V.tensor_tensor_scan(ends[:], groups[:], groups[:], 0.0, ALU.add, ALU.max))
                    link(V.tensor_tensor(base[:], ends[:], groups[:], ALU.subtract))
                    link(V.tensor_scalar(base[:], base[:], float(unit), -1.0, ALU.mult, ALU.add))
                    link(V.tensor_tensor(base[:PK], base[:PK], before[:PK], ALU.subtract))
                    link(V.tensor_tensor(base[:PK], base[:PK], below_ps[:PK, 0:K], ALU.add))
                    link(V.tensor_tensor(seen[:PK], seen[:PK], bc(base[:PK], 2, J), ALU.add))
                    link(V.tensor_tensor(seen[:PK], seen[:PK], mask[:PK], ALU.mult))
                    link(V.tensor_reduce(posf[:PK], seen[:PK].rearrange("p k j -> p j k"), AX, ALU.add))
                    link(V.tensor_copy(pos, posf[:PK]))
                    link(V.tensor_tensor(cmp[:], bc(cst["iota"][0:1, 0:ngroups], 2, K), bc(ends[0:1], 1, ngroups), ALU.is_ge))
                    link(V.tensor_reduce(gbf[:], cmp[:], AX, ALU.add))
                    link(V.tensor_scalar(group_bucket, gbf[:], float(K - 1), None, ALU.min))

            @block.tensor
            def _(pe):
                with guarded(pe, only_if):
                    pe.wait_ge(s_count, 1)
                    nc.tensor.matmul(below_ps[:, 0:K], cst["lower"][:PK, :], count[:PK], start=True, stop=True)
                    nc.tensor.matmul(total_ps[:, 0:K], cst["ones"][:PK, :], count[:PK], start=True, stop=True).then_inc(s_sums, 1)


def scatter_rows(nc, tag, pos, rows, table, PK, turns, B, clear=None, slots=2, only_if=None, sync_also=None):
    R = rows.shape[2]
    with ExitStack() as ctx:
        a = Pool_(nc, ctx, tag)
        ix = [a.sb(f"ix{s}", [P, B], I32) for s in range(slots)]
        rw = [a.sb(f"rw{s}", [P, B, R], rows.dtype) for s in range(slots)]
        s_full = [a.sem(f"full{s}") for s in range(slots)]
        s_free = [a.sem(f"free{s}") for s in range(slots)]
        s_clear, s_begin = a.sem("clear"), a.sem("begin")
        with nc.Block() as block:

            @block.sync
            def _(sp):
                with guarded(sp, only_if):
                    if clear is not None:
                        sp.dma_start(clear[0], clear[1]).then_inc(s_clear, 16)
                        sp.wait_ge(s_clear, 16)
                    if sync_also is not None:
                        sync_also(sp)

            @block.vector
            def _(dve):
                with guarded(dve, only_if):
                    def fill_slots(i, first=False):
                        for s in range(slots):
                            if not first:
                                dve.wait_ge(s_free[s], i * (16 * B))
                            at = i * (slots * B) + s * B
                            nc.vector.tensor_copy(ix[s][:PK], pos[:, bass.ds(at, B)]).then_inc(s_full[s], 1)
                            nc.vector.tensor_copy(rw[s][:PK], rows[:, bass.ds(at, B), :]).then_inc(s_full[s], 1)

                    fill_slots(0, first=True)
                    with dve.Fori(1, turns) as i:
                        fill_slots(i)

            @block.gpsimd
            def _(pool):
                with guarded(pool, only_if):
                    if clear is not None:
                        pool.wait_ge(s_clear, 16)
                    with pool.Fori(0, turns) as i:
                        for s in range(slots):
                            pool.wait_ge(s_full[s], (i + 1) * 2)
                            pool.sem_inc(s_begin, 1)
                            for b in range(B):
                                nc.gpsimd.indirect_dma_start(
                                    table, bass.IndirectOffsetOnAxis(ap=ix[s][:PK, b:b + 1], axis=0),
                                    rw[s][:PK, b, :], None).then_inc(s_free[s], 16)
                    for s in range(slots):
                        pool.wait_ge(s_free[s], 16 * B * turns)


def constants(nc, a, cst):
    ip = a.sb("ip", [P, 1])
    s_pool, s_chain = a.sem("pool"), a.sem("chain")
    with nc.Block() as block:

        @block.gpsimd
        def _(pool):
            nc.gpsimd.iota(cst["iota"][:], pattern=[[1, P]], base=0, channel_multiplier=0,
                           allow_small_or_imprecise_dtypes=True).then_inc(s_pool, 1)
            nc.gpsimd.iota(ip[:], pattern=[[0, 1]], base=0, channel_multiplier=1,
                           allow_small_or_imprecise_dtypes=True).then_inc(s_pool, 1)

        @block.vector
        def _(dve):
            link = Chain(dve, s_chain)
            dve.wait_ge(s_pool, 2)
            link(nc.vector.tensor_scalar(cst["lower"][:], cst["iota"][:], ip[:, 0:1], None, ALU.is_gt))
            link(nc.vector.tensor_scalar(cst["ident"][:], cst["iota"][:], ip[:, 0:1], None, ALU.is_equal))
            link(nc.vector.tensor_copy(cst["identb"][:], cst["ident"][:]))
            link(nc.vector.memset(cst["ones"][:], 1.0))


def edge_keys(nc, a, A, cst, ek, rec0, rec1, unsorted):
    src, dst = a.sb("src", [P, EJ], I32), a.sb("dst", [P, EJ], I32)
    w, attr = a.sb("w", [P, EJ]), a.sb("attr", [P, EJ, 3])
    part = a.sb("part", [P, EJ], I32)
    nxt, falls, falls_ps = a.sb("nxt", [P, EJ], I32), a.sb("falls", [P, 1]), a.ps("falls_ps", [P, 512])
    s_in, s_chain, s_next, s_falls, s_sum, s_clear = (a.sem(m) for m in ("in", "chain", "next", "falls", "sum", "clear"))
    with nc.Block() as block:

        @block.gpsimd
        def _(pool):
            nc.gpsimd.memset(nxt[:], N).then_inc(s_clear, 1)

        @block.sync
        def _(sp):
            for to, of in ((src, A["src"]), (dst, A["dst"]), (w, A["edge_weight"])):
                sp.dma_start(to[:EP], of.rearrange("(p j) -> p j", p=EP)).then_inc(s_in, 16)
            sp.dma_start(attr[:EP], A["edge_attr_3"].rearrange("(p j) c -> p j c", p=EP)).then_inc(s_in, 16)
            sp.wait_ge(s_clear, 1)
            last = (EP - 1) * EJ
            sp.dma_start(nxt[0:EP - 1], A["dst"][1:last + 1].rearrange("(p j) -> p j", j=EJ)).then_inc(s_next, 16)
            sp.dma_start(nxt[EP - 1:EP, 0:EJ - 1], A["dst"][last + 1:E].unsqueeze(0)).then_inc(s_next, 16)

        @block.vector
        def _(dve):
            link = Chain(dve, s_chain)
            V = nc.vector
            dve.wait_ge(s_in, 64)
            for k, (near, far, rec) in enumerate(((src, dst, rec0), (dst, src, rec1))):
                link(V.tensor_scalar(part[:EP], near[:EP], 7, None, ALU.arith_shift_right))
                link(V.tensor_copy(ek[k][:EP], part[:EP]))
                link(V.tensor_scalar(part[:EP], near[:EP], P - 1, None, ALU.bitwise_and))
                link(V.tensor_copy(rec[:EP, :, 1], part[:EP] if k == 0 else dst[:EP]))
                link(V.tensor_copy(rec[:EP, :, 0], far[:EP]))
            link(V.tensor_copy(rec0[:EP, :, 2], w[:EP]))
            link(V.memset(rec0[:EP, :, 3], 0.0))
            link(V.tensor_copy(rec1[:EP, :, 2:5], attr[:EP]))
            link(V.memset(rec1[:EP, :, 5], 1.0))
            link(V.memset(rec1[:EP, :, 6:8], 0.0))
            dve.wait_ge(s_next, 32)
            link(V.tensor_tensor(part[:EP], dst[:EP], nxt[:EP], ALU.is_gt))
            link(V.tensor_copy(w[:EP], part[:EP]))
            V.tensor_reduce(falls[:EP], w[:EP], AX, ALU.max).then_inc(s_falls, 1)
            dve.wait_ge(s_sum, 1)
            link(V.tensor_copy(unsorted[:], falls_ps[0:1, 0:1]))

        @block.tensor
        def _(pe):
            pe.wait_ge(s_falls, 1)
            nc.tensor.matmul(falls_ps[0:1, 0:1], cst["ones"][:EP, 0:1], falls[:EP], start=True, stop=True).then_inc(s_sum, 1)


def order_edges(nc, cst, key, rec, table, pos, unsorted):
    only_if = unsorted[0:1, 0:1]
    s_store = nc.alloc_semaphore("order_store")
    with nc.Block() as block:

        @block.sync
        def _(sp):
            sp.dma_start(table[0:E].rearrange("(p j) r -> p j r", p=EP), rec[:EP]).then_inc(s_store, 16)
            sp.wait_ge(s_store, 16)

    spent.append(s_store)
    for shift, K in ((0, 16), (4, 8), (7, NT)):
        with ExitStack() as ctx:
            a = Pool_(nc, ctx, f"place{shift}")
            part, digit = a.sb("part", [P, EJ], I32), a.sb("digit", [P, EJ])
            s_chain, s_back = a.sem("chain"), a.sem("back")
            with nc.Block() as block:

                @block.vector
                def _(dve):
                    with guarded(dve, only_if):
                        link, V = Chain(dve, s_chain), nc.vector
                        link(V.tensor_copy(part[:EP], rec[:EP, :, 1]))
                        link(V.tensor_scalar(part[:EP], part[:EP], shift, (1 << K.bit_length()) - 1 if K == NT else K - 1,
                                             ALU.arith_shift_right, ALU.bitwise_and))
                        link(V.tensor_copy(digit[:EP], part[:EP]))

            sort_positions(nc, f"psort{shift}", cst, digit[:EP], EP, EJ, K, 1, pos[:EP], 1, part[0:1, 0:1], only_if=only_if)
            scatter_rows(nc, f"pscat{shift}", pos[:EP], rec[:EP], table, EP, 25, 8, only_if=only_if)
            with nc.Block() as block:

                @block.sync
                def _(sp):
                    with guarded(sp, only_if):
                        sp.dma_start(rec[:EP], table[0:E].rearrange("(p j) r -> p j r", p=EP)).then_inc(s_back, 16)
                        sp.wait_ge(s_back, 16)


def load_groups(nc, cst, key, table, tile, group_bucket, bucket, scatter):
    K = NT
    with ExitStack() as ctx:
        a = Pool_(nc, ctx, "groups")
        mask = a.sb("mask", [P, K, EJ])
        count, ti, groups, ends, total, base = (a.sb(m, [P, K], I32 if m == "ti" else F32)
                                                for m in ("count", "ti", "groups", "ends", "total", "base"))
        cmp, start = a.sb("cmp", [P, NG, K]), a.sb("start", [P, NG])
        starti = a.sb("starti", [1, NG], I32)
        total_ps = a.ps("total_ps", [P, 512])
        s_chain, s_count, s_sums, s_tile = (a.sem(m) for m in ("chain", "count", "sums", "tile"))
        with nc.Block() as block:

            @block.vector
            def _(dve):
                link, V = Chain(dve, s_chain), nc.vector
                link(V.tensor_tensor(mask[:EP], bc(key[:EP], 1, K), bc(cst["iota"][:EP, 0:K], 2, EJ), ALU.is_equal))
                V.tensor_reduce(count[:EP], mask[:EP], AX, ALU.add).then_inc(s_count, 1)
                dve.wait_ge(s_sums, 1)
                link(V.tensor_copy(total[:], total_ps[:, 0:K]))
                link(V.tensor_scalar(ti[:], total[:], float(GE - 1), None, ALU.add))
                link(V.tensor_scalar(ti[:], ti[:], GE.bit_length() - 1, None, ALU.arith_shift_right))
                link(V.tensor_copy(groups[:], ti[:]))
                link(V.tensor_tensor_scan(ends[:], groups[:], groups[:], 0.0, ALU.add, ALU.max))
                link(V.tensor_tensor_scan(base[:], total[:], total[:], 0.0, ALU.add, ALU.max))
                link(V.tensor_tensor(base[:], base[:], total[:], ALU.subtract))
                link(V.tensor_tensor(groups[:], ends[:], groups[:], ALU.subtract))
                link(V.scalar_tensor_tensor(base[:], groups[:], -float(GE), base[:], ALU.mult, ALU.add))
                link(V.tensor_tensor(cmp[:], bc(cst["iota"][:, 0:NG], 2, K), bc(ends[:], 1, NG), ALU.is_ge))
                link(V.tensor_reduce(bucket[:], cmp[:], AX, ALU.add))
                link(V.tensor_scalar(bucket[:], bucket[:], float(K - 1), None, ALU.min))
                link(V.tensor_copy(group_bucket, bucket[0:1, :]))
                link(V.tensor_tensor(cmp[:], bc(bucket[:], 2, K), bc(cst["iota"][:, 0:K], 1, NG), ALU.is_equal))
                link(V.tensor_tensor(cmp[:], cmp[:], bc(base[:], 1, NG), ALU.mult))
                link(V.tensor_reduce(start[:], cmp[:], AX, ALU.add))
                link(V.scalar_tensor_tensor(start[:], cst["iota"][:, 0:NG], float(GE), start[:], ALU.mult, ALU.add))
                link(V.tensor_scalar(starti[:], start[0:1, :], float(E), None, ALU.min))

            @block.tensor
            def _(pe):
                pe.wait_ge(s_count, 1)
                nc.tensor.matmul(total_ps[:, 0:K], cst["ones"][:EP, :], count[:EP], start=True, stop=True).then_inc(s_sums, 1)

        def loads(sp):
            with sp.Fori(0, NG) as g:
                at = sp.value_load(starti[0:1, bass.ds(g, 1)], min_val=0, max_val=E)
                sp.dma_start(tile[:, bass.ds(g, 1), :].rearrange("p a x -> p (a x)"),
                             table[bass.ds(at, GE), :].rearrange("(p q) r -> p (q r)", p=P)).then_inc(s_tile, 16)
            sp.wait_ge(s_tile, 16 * NG)

        scatter(loads)
    with ExitStack() as ctx:
        a = Pool_(nc, ctx, "places")
        low, inb = a.sb("low", [P, NG, G]), a.sb("inb", [P, NG, G])
        s_chain = a.sem("chain")
        with nc.Block() as block:

            @block.vector
            def _(dve):
                link, V = Chain(dve, s_chain), nc.vector
                rows = tile.rearrange("p g (q r) -> p g q r", r=8)
                place, real = rows[:, :, :, 1], rows[:, :, :, 5]
                link(V.tensor_scalar(bucket[:], bucket[:], -float(P), None, ALU.mult))
                link(V.tensor_tensor(low[:], place, bc(bucket[:], 2, G), ALU.add))
                link(V.tensor_copy(place, low[:]))
                link(V.tensor_scalar(inb[:], low[:], 0.0, None, ALU.is_ge))
                link(V.tensor_tensor(real, real, inb[:], ALU.mult))
                link(V.tensor_scalar(inb[:], low[:], float(P), None, ALU.is_lt))
                link(V.tensor_tensor(real, real, inb[:], ALU.mult))


def load_sorted(nc, a, tables, tiles):
    s_in = a.sem("in")
    with nc.Block() as block:

        @block.sync
        def _(sp):
            for t, (table, tile) in enumerate(zip(tables, tiles)):
                sp.dma_start(tile[:], table.rearrange("(g p q) r -> p g (q r)", p=P, q=G)).then_inc(s_in, 16)
            sp.wait_ge(s_in, 16 * len(tables))



TB = 5
TURNS = NT // TB
HW = H * (D + 1)
HR = HW + H
HN = C + H
PF = 10


def load_nodes(nc, a, x_dram, x):
    s_zero, s_in = a.sem("zero"), a.sem("in")
    full = (NT - 1) * P
    with nc.Block() as block:

        @block.vector
        def _(dve):
            nc.vector.memset(x[:, NT - 1, :], 0.0).then_inc(s_zero, 1)

        @block.sync
        def _(sp):
            sp.dma_start(x[:, 0:NT - 1, :], x_dram[0:full].rearrange("(t p) c -> p t c", p=P)).then_inc(s_in, 16)
            sp.wait_ge(s_zero, 1)
            sp.dma_start(x[0:N - full, NT - 1, :], x_dram[full:N]).then_inc(s_in, 16)
            sp.wait_ge(s_in, 32)


def store_nodes(nc, a, x, x_dram):
    s_out = a.sem("out")
    full = (NT - 1) * P
    with nc.Block() as block:

        @block.sync
        def _(sp):
            sp.dma_start(x_dram[0:full].rearrange("(t p) c -> p t c", p=P), x[:, 0:NT - 1, :]).then_inc(s_out, 16)
            sp.dma_start(x_dram[full:N], x[0:N - full, NT - 1, :]).then_inc(s_out, 16)
            sp.wait_ge(s_out, 32)


def layernorm(nc, tag, x, y, table=None):
    def tile(of, i, b):
        return of[:, bass.ds(i * TB + b, 1), :].rearrange("p a c -> p (a c)")

    with ExitStack() as ctx:
        a = Pool_(nc, ctx, tag)
        st = a.sb("st", [P, NT, 6])
        mean, var, t0 = a.sb("mean", [P, NT]), a.sb("var", [P, NT]), a.sb("t0", [P, NT])
        s_stats, s_chain, s_var, s_std = a.sem("stats"), a.sem("chain"), a.sem("var"), a.sem("std")
        s_y, s_out = a.sem("y"), a.sem("out")
        with nc.Block() as block:

            @block.vector
            def _(dve):
                link, V = Chain(dve, s_chain), nc.vector
                with dve.Fori(0, TURNS) as i:
                    for b in range(TB):
                        V.bn_stats(tile(st, i, b), tile(x, i, b)).then_inc(s_stats, 1)
                dve.wait_ge(s_stats, NT)
                link(V.tensor_tensor(mean[:], st[:, :, 1], st[:, :, 4], ALU.add))
                link(V.tensor_scalar(mean[:], mean[:], 0.5, None, ALU.mult))
                link(V.tensor_tensor(var[:], st[:, :, 1], st[:, :, 4], ALU.subtract))
                link(V.tensor_tensor(var[:], var[:], var[:], ALU.mult))
                link(V.tensor_tensor(t0[:], st[:, :, 2], st[:, :, 5], ALU.add))
                link(V.tensor_scalar(t0[:], t0[:], 1.0 / C, EPS, ALU.mult, ALU.add))
                V.scalar_tensor_tensor(var[:], var[:], 0.25, t0[:], ALU.mult, ALU.add).then_inc(s_var, 1)
                dve.wait_ge(s_std, 1)
                link(V.reciprocal(t0[:], t0[:]))
                with dve.Fori(0, TURNS) as i:
                    for b in range(TB):
                        V.tensor_scalar(tile(y, i, b), tile(x, i, b), mean[:, bass.ds(i * TB + b, 1)],
                                        t0[:, bass.ds(i * TB + b, 1)], ALU.subtract, ALU.mult).then_inc(s_y, 1)

            @block.scalar
            def _(act):
                act.wait_ge(s_var, 1)
                nc.scalar.activation(t0[:], var[:], ACT.Sqrt).then_inc(s_std, 1)

            @block.sync
            def _(sp):
                if table is not None:
                    sp.wait_ge(s_y, NT)
                    sp.dma_start(table.rearrange("(t p) c -> p t c", p=P), y[:]).then_inc(s_out, 16)
                    sp.wait_ge(s_out, 16)


def project(nc, tag, cst, w, width, prep, preps, evac, evacs):
    with ExitStack() as ctx:
        a = Pool_(nc, ctx, tag)
        xs, xt = a.sb("xs", [P, TB, C]), a.sb("xt", [P, TB, C])
        turned, product = a.ps("turned", [P, TB + 1, C]), a.ps("product", [P, TB + 1, C])
        s_chain, s_xs, s_turned = a.sem("chain"), a.sem("xs"), a.sem("turned")
        s_xt, s_product, s_took = a.sem("xt"), a.sem("product"), a.sem("took")
        with nc.Block() as block:

            @block.vector
            def _(dve):
                link = Chain(dve, s_chain)

                def rows(i):
                    prep(link, i, xs)
                    dve.sem_inc(s_xs, 1)

                def results(i):
                    dve.wait_ge(s_product, i + 1)
                    evac(link, i, product)
                    dve.sem_inc(s_took, 1)

                rows(0)
                with dve.Fori(0, TURNS - 1) as i:
                    link.turn(i, preps + evacs)
                    dve.wait_ge(s_turned, i + 1)
                    rows(i + 1)
                    results(i)
                link.end(TURNS - 1)
                results(TURNS - 1)

            @block.tensor
            def _(pe):
                def turn(i, first=False):
                    pe.wait_ge(s_xs, i + 1)
                    for b in range(TB):
                        for k in range(KC):
                            last = nc.tensor.transpose(turned[:, b, k * P:(k + 1) * P],
                                                       xs[:, b, k * P:(k + 1) * P], cst["ident"][:])
                    last.then_inc(s_turned, 1)
                    pe.wait_ge(s_xt, i + 1)
                    if not first:
                        pe.wait_ge(s_took, i)
                    for b in range(TB):
                        for k in range(KC):
                            last = nc.tensor.matmul(product[:, b, 0:width], xt[:, b, k * P:(k + 1) * P],
                                                    w[:, k, 0:width], start=(k == 0), stop=(k == KC - 1))
                    last.then_inc(s_product, 1)

                turn(0, first=True)
                with pe.Fori(1, TURNS) as i:
                    turn(i)

            @block.scalar
            def _(act):
                with act.Fori(0, TURNS) as i:
                    act.wait_ge(s_turned, i + 1)
                    nc.scalar.copy(xt[:], turned[:, 0:TB, :]).then_inc(s_xt, 1)


def gather_sum(nc, cst, sorted0, gb, table, agg):
    with ExitStack() as ctx:
        a = Pool_(nc, ctx, "gsum")
        two, four = range(2), range(4)
        ix = [a.sb(f"ix{s}", [P, G], I32) for s in four]
        rows = [a.sb(f"rows{s}", [P, G, C]) for s in four]
        rc = [a.sb(f"rc{s}", [P, G, 4]) for s in two]
        hot = [a.sb(f"hot{s}", [P, G, P]) for s in two]
        part = [a.ps(f"part{s}", [P, 512]) for s in two]
        s_chain, s_ix, s_hot, s_mm, s_go = (a.sem(m) for m in ("chain", "ix", "hot", "mm", "go"))
        s_rows = [a.sem(f"rows{s}") for s in four]
        LOOPED = (NG - 4) // 4

        with nc.Block() as block:

            @block.vector
            def _(dve):
                link, V = Chain(dve, s_chain), nc.vector

                def record(g):
                    return sorted0[:, bass.ds(g, 1), :].rearrange("p a (q r) -> p (a q) r", r=4)

                def index(g, k):
                    V.tensor_copy(ix[k % 4][:], record(g)[:, :, 0]).then_inc(s_ix, 1)

                def prepare(g, k):
                    link(V.tensor_copy(rc[k % 2][:], record(g)))
                    for q in range(G):
                        last = V.tensor_scalar(hot[k % 2][:, q, :], cst["iota"][:], rc[k % 2][:, q, 1:2],
                                               rc[k % 2][:, q, 2:3], ALU.is_equal, ALU.mult)
                    last.then_inc(s_hot, 1)

                def take(g, k):
                    b = dve.value_load(gb[0:1, bass.ds(g, 1)], min_val=0, max_val=NT - 1)
                    dve.wait_ge(s_mm, g + 1)
                    to = agg[:, bass.ds(b, 1), :].rearrange("p a c -> p (a c)")
                    link(V.tensor_tensor(to, to, part[k % 2][:, 0:C], ALU.add))

                link(V.memset(agg[:], 0.0))
                for g in range(4):
                    index(g, g)
                prepare(0, 0)
                with dve.Fori(0, LOOPED) as i:
                    link.turn(i, 8)
                    for k in range(4):
                        prepare(i * 4 + k + 1, k + 1)
                        take(i * 4 + k, k)
                        index(i * 4 + k + 4, k)
                link.end(LOOPED)
                for g in range(4 * LOOPED, NG):
                    if g + 1 < NG:
                        prepare(g + 1, g + 1)
                    take(g, g)
                    if g + 4 < NG:
                        index(g + 4, g)

            @block.gpsimd
            def _(pool):
                def gather(g, k):
                    pool.wait_ge(s_ix, g + 1)
                    pool.sem_inc(s_go, 1)
                    for q in range(G):
                        nc.gpsimd.indirect_dma_start(
                            rows[k % 4][:, q, :], None, table,
                            bass.IndirectOffsetOnAxis(ap=ix[k % 4][:, q:q + 1], axis=0)).then_inc(s_rows[k % 4], 16)

                with pool.Fori(0, NG // 4) as i:
                    for k in range(4):
                        gather(i * 4 + k, k)
                for g in range(NG // 4 * 4, NG):
                    gather(g, g)

            @block.tensor
            def _(pe):
                def products(g, k, i):
                    pe.wait_ge(s_hot, g + 1)
                    pe.wait_ge(s_rows[k % 4], (i + 1) * (16 * G))
                    for q in range(G):
                        last = nc.tensor.matmul(part[k % 2][:, 0:C], hot[k % 2][:, q, :], rows[k % 4][:, q, :],
                                                start=(q == 0), stop=(q == G - 1))
                    last.then_inc(s_mm, 1)

                with pe.Fori(0, NG // 4) as i:
                    for k in range(4):
                        products(i * 4 + k, k, i)
                for g in range(NG // 4 * 4, NG):
                    products(g, g, g // 4)


def row_broadcast(sp, to, vec, sem):
    sp.dma_start(to, vec.unsqueeze(0).broadcast_to([P] + list(vec.shape))).then_inc(sem, 16)


def gnn0(nc, cst, A, x, n, agg):
    with ExitStack() as ctx:
        a = Pool_(nc, ctx, "gnn0")
        w, dg, bi = a.sb("w", [P, KC, C]), a.sb("dg", [P, C]), a.sb("bi", [P, C])
        s_in, s_dg = a.sem("in"), a.sem("dg")
        with nc.Block() as block:

            @block.sync
            def _(sp):
                row_broadcast(sp, dg[:], A["L0_gnn_learnable_diag"], s_in)
                row_broadcast(sp, bi[:], A["L0_gnn_bias"], s_in)
                sp.dma_start(w[:], A["L0_gnn_weight"].rearrange("(k p) c -> p k c", p=P)).then_inc(s_in, 16)

            @block.vector
            def _(dve):
                dve.wait_ge(s_in, 48)
                nc.vector.tensor_scalar(dg[:], dg[:], 1.0, None, ALU.add).then_inc(s_dg, 1)

        V = nc.vector

        def prep(link, i, xs):
            at = bass.ds(i * TB, TB)
            link(V.tensor_tensor(xs[:], agg[:, at, :], bc(dg[:], 1, TB), ALU.mult))
            link(V.tensor_tensor(xs[:], n[:, at, :], xs[:], ALU.subtract))

        def evac(link, i, ps):
            to = x[:, bass.ds(i * TB, TB), :]
            link(V.tensor_tensor(to, to, ps[:, 0:TB, :], ALU.add))
            link(V.tensor_tensor(to, to, bc(bi[:], 1, TB), ALU.add))

        project(nc, "gnn0p", cst, w, C, prep, 2, evac, 2)

def gate(nc, tag, cst, logits, K, keys, weights):
    ranks = len(weights)
    with ExitStack() as ctx:
        a = Pool_(nc, ctx, tag)
        top = [a.sb(f"top{r}", [P, NT]) for r in range(ranks)]
        eq, rev = a.sb("eq", [P, NT, K]), a.sb("rev", [P, K])
        s_chain, s_arg, s_exp = a.sem("chain"), a.sem("arg"), a.sem("exp")
        with nc.Block() as block:

            @block.vector
            def _(dve):
                link, V = Chain(dve, s_chain), nc.vector
                link(V.tensor_scalar(rev[:], cst["iota"][:, 0:K], -1.0, float(K), ALU.mult, ALU.add))
                for r in range(ranks):
                    key = keys[:, r * NT:(r + 1) * NT]
                    link(V.tensor_reduce(top[r][:], logits[:], AX, ALU.max))
                    link(V.tensor_tensor(eq[:], logits[:], bc(top[r][:], 2, K), ALU.is_equal))
                    link(V.tensor_tensor(eq[:], eq[:], bc(rev[:], 1, NT), ALU.mult))
                    link(V.tensor_reduce(key, eq[:], AX, ALU.max))
                    link(V.tensor_scalar(key, key, -1.0, float(K), ALU.mult, ALU.add))
                    if r < ranks - 1:
                        link(V.tensor_tensor(eq[:], bc(cst["iota"][:, 0:K], 1, NT), bc(key, 2, K), ALU.is_equal))
                        link(V.scalar_tensor_tensor(logits[:], eq[:], -BIG, logits[:], ALU.mult, ALU.add))
                if ranks == 2:
                    V.tensor_tensor(top[1][:], top[1][:], top[0][:], ALU.subtract).then_inc(s_arg, 1)
                    dve.wait_ge(s_exp, 1)
                    link(V.tensor_scalar(weights[0], top[1][:], 1.0, None, ALU.add))
                    link(V.reciprocal(weights[0], weights[0]))
                    link(V.tensor_tensor(weights[1], top[1][:], weights[0], ALU.mult))
                else:
                    V.tensor_tensor(logits[:], logits[:], bc(top[0][:], 2, K), ALU.subtract).then_inc(s_arg, 1)
                    dve.wait_ge(s_exp, 1)
                    link(V.tensor_reduce(weights[0], logits[:], AX, ALU.add))
                    link(V.reciprocal(weights[0], weights[0]))

            @block.scalar
            def _(act):
                act.wait_ge(s_arg, 1)
                to = top[1] if ranks == 2 else logits
                nc.scalar.activation(to[:], to[:], ACT.Exp).then_inc(s_exp, 1)


def route(nc, tag, cst, keys, ranks, K, tiles, B, pos, experts, tokens, table):
    J = ranks * NT
    with ExitStack() as ctx:
        a = Pool_(nc, ctx, tag)
        ids, fill = a.sb("ids", [P, J, 1]), a.sb("fill", [P, tiles])
        sort_positions(nc, tag + "s", cst, keys[:], P, J, K, P, pos[:], tiles, experts[:])
        s_ids, s_chain = a.sem("ids"), a.sem("chain")
        with nc.Block() as block:

            @block.gpsimd
            def _(pool):
                for r in range(ranks):
                    nc.gpsimd.iota(ids[:, r * NT:(r + 1) * NT, 0], pattern=[[P, NT]], base=0, channel_multiplier=1,
                                   allow_small_or_imprecise_dtypes=True).then_inc(s_ids, 1)
                nc.gpsimd.memset(fill[:], 0.0).then_inc(s_ids, 1)
                pool.wait_ge(s_ids, ranks + 1)

        scatter_rows(nc, tag + "w", pos[:], ids[:], table, P, J // (ranks * B), B,
                     (table.rearrange("(p t) r -> p (t r)", p=P), fill[:]), slots=ranks)
        by_tile, turned = a.sb("by_tile", [tiles, P]), a.ps("turned", [P, 512])
        s_in, s_turned = a.sem("in"), a.sem("turned")
        with nc.Block() as block:

            @block.sync
            def _(sp):
                sp.dma_start(by_tile[:], table.rearrange("(t p) r -> t (p r)", p=P)).then_inc(s_in, 16)

            @block.tensor
            def _(pe):
                pe.wait_ge(s_in, 16)
                nc.tensor.transpose(turned[:, 0:tiles], by_tile[:], cst["ident"][0:tiles, 0:tiles]).then_inc(s_turned, 1)

            @block.vector
            def _(dve):
                dve.wait_ge(s_turned, 1)
                nc.vector.tensor_copy(tokens[:], turned[:, 0:tiles]).then_inc(s_chain, 1)


def run_experts(nc, tag, cst, tiles, experts, tokens, rows_table, w1, w1_fixed, b1t, b1_fixed, FC, w2, b2, func, ytable):
    F = FC * P
    HB = (F + 511) // 512
    with ExitStack() as ctx:
        a = Pool_(nc, ctx, tag)
        two = range(2)
        ix = [a.sb(f"ix{s}", [P, 1], I32) for s in two]
        rows = [a.sb(f"rows{s}", [P, C]) for s in two]
        xt = [a.sb(f"xt{s}", [P, C]) for s in two]
        w1s = [a.sb(f"w1s{s}", [P, KC, F]) for s in two] if w1_fixed is None else [w1_fixed] * 2
        w2s = [a.sb(f"w2s{s}", [P, FC, C]) for s in two]
        ht = [a.sb(f"ht{s}", [P, FC, P]) for s in two]
        ys = [a.sb(f"ys{s}", [P, C]) for s in two]
        turned = a.ps("turned", [P, 512])
        hidden = [a.ps(f"hidden{s}", [P, HB * 512]) for s in two]
        y = [a.ps(f"y{s}", [P, 512]) for s in two]
        s_ix, s_turned, s_xt, s_hidden, s_ht, s_y, s_ys = (
            a.sem(m) for m in ("ix", "turned", "xt", "hidden", "ht", "y", "ys"))
        s_rows, s_w1, s_w2, s_out = ([a.sem(f"{m}{s}") for s in two] for m in ("rows", "w1", "w2", "out"))
        s_go = a.sem("go")

        def tiles_by_two(eng, step):
            step(0, 0)
            step(1, 1)
            with eng.Fori(1, tiles // 2) as i:
                step(i * 2, 0)
                step(i * 2 + 1, 1)
            if tiles % 2:
                step(tiles - 1, 0)

        def pipelined(eng, step):
            step(0, 0, 0)
            step(1, 1, 0)
            looped = (tiles - 4) // 2
            with eng.Fori(1, looped) as i:
                step(i * 2, 0, i)
                step(i * 2 + 1, 1, i)
            for t in range(2 * looped, tiles):
                step(t, t % 2, t // 2)

        def early(t):
            return isinstance(t, int) and t < 2

        with nc.Block() as block:

            @block.sync
            def _(sp):
                def load(t, s):
                    e = sp.value_load(experts[0:1, bass.ds(t, 1)], min_val=0, max_val=w2.shape[0] - 1)
                    if w1_fixed is None:
                        if not early(t):
                            sp.wait_ge(s_hidden, t - 1)
                        sp.dma_start(w1s[s][:], w1[bass.ds(e, 1)].rearrange("a (k p) f -> p (a k) f", p=P)).then_inc(s_w1[s], 16)
                    if not early(t):
                        sp.wait_ge(s_y, t - 1)
                    sp.dma_start(w2s[s][:], w2[bass.ds(e, 1)].rearrange("a (k p) c -> p (a k) c", p=P)).then_inc(s_w2[s], 16)

                tiles_by_two(sp, load)

            @block.gpsimd
            def _(pool):
                def gather(t, s):
                    pool.wait_ge(s_ix, t + 1)
                    pool.sem_inc(s_go, 1)
                    if not early(t):
                        pool.wait_ge(s_turned, t - 1)
                        pool.sem_inc(s_go, 1)
                    nc.gpsimd.indirect_dma_start(
                        rows[s][:], None, rows_table,
                        bass.IndirectOffsetOnAxis(ap=ix[s][:, 0:1], axis=0)).then_inc(s_rows[s], 16)

                tiles_by_two(pool, gather)

            @block.vector
            def _(dve):
                V = nc.vector

                def index(t, s):
                    V.tensor_copy(ix[s][:], tokens[:, bass.ds(t, 1)]).then_inc(s_ix, 1)

                def take(t, s, i):
                    e = dve.value_load(experts[0:1, bass.ds(t, 1)], min_val=0, max_val=w2.shape[0] - 1)
                    dve.wait_ge(s_y, t + 1)
                    if not early(t):
                        dve.wait_ge(s_out[s], i * 16)
                    V.tensor_tensor(ys[s][:], y[s][:, 0:C], b2[:, bass.ds(e, 1), :].rearrange("p a c -> p (a c)"),
                                    ALU.add).then_inc(s_ys, 1)

                def step(t, s, i):
                    if not isinstance(t, int) or t + 4 < tiles:
                        dve.wait_ge(s_turned, t + 3)
                        index(t + 4, s)
                    take(t, s, i)

                index(0, 0)
                index(1, 1)
                for t in (2, 3):
                    dve.wait_ge(s_turned, t - 1)
                    index(t, t % 2)
                pipelined(dve, step)

            @block.tensor
            def _(pe):
                def turn(t, s, n):
                    pe.wait_ge(s_rows[s], n * 16)
                    for k in range(KC):
                        last = nc.tensor.transpose(turned[:, k * P:(k + 1) * P], rows[s][:, k * P:(k + 1) * P],
                                                   cst["ident"][:])
                    last.then_inc(s_turned, 1)

                def first_products(t, s, n):
                    pe.wait_ge(s_xt, t + 1)
                    if w1_fixed is None:
                        pe.wait_ge(s_w1[s], n * 16)
                    for f in range(FC):
                        for k in range(KC):
                            last = nc.tensor.matmul(hidden[s][:, f * P:(f + 1) * P], w1s[s][:, k, f * P:(f + 1) * P],
                                                    xt[s][:, k * P:(k + 1) * P], start=(k == 0), stop=(k == KC - 1))
                    last.then_inc(s_hidden, 1)

                def second_products(t, s, n):
                    pe.wait_ge(s_ht, t + 1)
                    pe.wait_ge(s_w2[s], n * 16)
                    if not early(t):
                        pe.wait_ge(s_ys, t - 1)
                    for f in range(FC):
                        last = nc.tensor.matmul(y[s][:, 0:C], ht[s][:, f, :], w2s[s][:, f, :],
                                                start=(f == 0), stop=(f == FC - 1))
                    last.then_inc(s_y, 1)

                def step(t, s, i):
                    late = not isinstance(t, int)
                    if late or t + 1 < tiles:
                        first_products(t + 1, 1 - s, i + 1 + s)
                    if late or t + 2 < tiles:
                        turn(t + 2, s, i + 2)
                    second_products(t, s, i + 1)

                turn(0, 0, 1)
                first_products(0, 0, 1)
                turn(1, 1, 1)
                pipelined(pe, step)

            @block.scalar
            def _(act):
                def copy_rows(t, s):
                    act.wait_ge(s_turned, t + 1)
                    nc.scalar.copy(xt[s][:], turned[:, 0:C]).then_inc(s_xt, 1)

                def units(t, s):
                    e = 0 if b1_fixed else act.value_load(experts[0:1, bass.ds(t, 1)], min_val=0, max_val=w2.shape[0] - 1)
                    act.wait_ge(s_hidden, t + 1)
                    for f in range(FC):
                        bias = b1t[:, 0, f:f + 1] if b1_fixed else b1t[:, bass.ds(e, 1), f:f + 1].rearrange("p a b -> p (a b)")
                        last = nc.scalar.activation(ht[s][:, f, :], hidden[s][:, f * P:(f + 1) * P], func, bias=bias)
                    last.then_inc(s_ht, 1)

                def store(t, s):
                    act.wait_ge(s_ys, t + 1)
                    nc.scalar.dma_start(ytable[bass.ds(t * P, P), :], ys[s][:]).then_inc(s_out[s], 16)

                def step(t, s, i):
                    late = not isinstance(t, int)
                    units(t, s)
                    if late or t + 2 < tiles:
                        copy_rows(t + 2, s)
                    if late or t > 0:
                        store(t - 1, 1 - s)

                copy_rows(0, 0)
                copy_rows(1, 1)
                pipelined(act, step)
                store(tiles - 1, (tiles - 1) % 2)
                act.wait_ge(s_out[0], (tiles + 1) // 2 * 16)
                act.wait_ge(s_out[1], tiles // 2 * 16)


def fetch(nc, a, pos, J, ytable, got):
    s_got = a.sem("got")
    with nc.Block() as block:

        @block.gpsimd
        def _(pool):
            for j in range(J):
                nc.gpsimd.indirect_dma_start(got[:, j, :], None, ytable,
                                             bass.IndirectOffsetOnAxis(ap=pos[:, j:j + 1], axis=0)).then_inc(s_got, 16)
            pool.wait_ge(s_got, 16 * J)


def load_biases(nc, a, cst, b1, b1t, b2, b2b):
    rows = b1.shape[0] * b1.shape[1] // P
    flat, turned = a.sb("flat", [rows, P]), a.ps("turned", [P, 512])
    s_in, s_turned, s_done = a.sem("in"), a.sem("turned"), a.sem("done")
    with nc.Block() as block:

        @block.sync
        def _(sp):
            sp.dma_start(flat[:], b1.rearrange("e (f p) -> (e f) p", p=P)).then_inc(s_in, 16)
            row_broadcast(sp, b2b[:], b2, s_done)
            sp.wait_ge(s_done, 16)

        @block.tensor
        def _(pe):
            pe.wait_ge(s_in, 16)
            nc.tensor.transpose(turned[:, 0:rows], flat[:], cst["ident"][0:rows, 0:rows]).then_inc(s_turned, 1)

        @block.scalar
        def _(act):
            act.wait_ge(s_turned, 1)
            nc.scalar.copy(b1t[:].rearrange("p e f -> p (e f)"), turned[:, 0:rows]).then_inc(s_turned, 1)


def ffn0(nc, cst, A, x, n, ntab):
    ytab = nc.dram_tensor("ytab0", (S0 * P, C), F32, kind="Internal").ap()
    rtab = nc.dram_tensor("rtab0", (S0 * P, 1), F32, kind="Internal").ap()
    J = 2 * NT
    with ExitStack() as ctx:
        a = Pool_(nc, ctx, "ffn0")
        wt = [a.sb(f"wt{r}", [P, NT]) for r in range(2)]
        pos = a.sb("pos", [P, J], I32)
        with ExitStack() as c1:
            b = Pool_(nc, c1, "ffn0g")
            wg, bg = b.sb("wg", [P, KC, E0]), b.sb("bg", [P, E0])
            logits, keys = b.sb("logits", [P, NT, E0]), b.sb("keys", [P, J])
            experts, tokens = b.sb("experts", [1, S0], I32), b.sb("tokens", [P, S0], I32)
            b1t, b2b = b.sb("b1t", [P, E0, FC0]), b.sb("b2b", [P, E0, C])
            s_in = b.sem("in")
            with nc.Block() as block:

                @block.sync
                def _(sp):
                    sp.dma_start(wg[:], A["L0_ffn_gate_w"].rearrange("(k p) e -> p k e", p=P)).then_inc(s_in, 16)
                    row_broadcast(sp, bg[:], A["L0_ffn_gate_b"], s_in)
                    sp.wait_ge(s_in, 32)

            V = nc.vector

            def prep(link, i, xs):
                link(V.tensor_copy(xs[:], n[:, bass.ds(i * TB, TB), :]))

            def evac(link, i, ps):
                link(V.tensor_tensor(logits[:, bass.ds(i * TB, TB), :], ps[:, 0:TB, 0:E0], bc(bg[:], 1, TB), ALU.add))

            project(nc, "gate0p", cst, wg, E0, prep, 1, evac, 1)
            gate(nc, "gate0", cst, logits, E0, keys, [w[:] for w in wt])
            route(nc, "route0", cst, keys, 2, E0, S0, 5, pos, experts, tokens, rtab)
            with ExitStack() as c2:
                load_biases(nc, Pool_(nc, c2, "bias0"), cst, A["L0_ffn_b1"], b1t, A["L0_ffn_b2"], b2b)
            run_experts(nc, "exp0", cst, S0, experts, tokens, ntab, A["L0_ffn_w1"], None, b1t, False, FC0,
                        A["L0_ffn_w2"], b2b, ACT.Relu, ytab)
        with ExitStack() as c1:
            b = Pool_(nc, c1, "ffn0c")
            got = b.sb("got", [P, J, C])
            fetch(nc, b, pos, J, ytab, got)
            gb2 = b.sb("gb2", [P, 2, C])
            s_in, s_chain = b.sem("in"), b.sem("chain")
            with nc.Block() as block:

                @block.vector
                def _(dve):
                    link, V = Chain(dve, s_chain), nc.vector
                    for r in range(2):
                        part = got[:, r * NT:(r + 1) * NT, :]
                        link(V.tensor_tensor(part, part, bc(wt[r][:], 2, C), ALU.mult))
                    link(V.tensor_tensor(got[:, 0:NT, :], got[:, 0:NT, :], got[:, NT:J, :], ALU.add))
                    link(V.tensor_tensor(n[:], n[:], got[:, 0:NT, :], ALU.add))

            layernorm(nc, "lnm", n, got[:, 0:NT, :])
            with nc.Block() as block:

                @block.sync
                def _(sp):
                    row_broadcast(sp, gb2[:, 0, :], A["L0_ffn_gamma"], s_in)
                    row_broadcast(sp, gb2[:, 1, :], A["L0_ffn_beta"], s_in)

                @block.vector
                def _(dve):
                    link, V = Chain(dve, s_chain), nc.vector
                    link.n = 4
                    dve.wait_ge(s_in, 32)
                    y = got[:, 0:NT, :]
                    link(V.tensor_tensor(y, y, bc(gb2[:, 0, :], 1, NT), ALU.mult))
                    link(V.tensor_tensor(y, y, bc(gb2[:, 1, :], 1, NT), ALU.add))
                    link(V.tensor_tensor(x[:], x[:], y, ALU.add))


def ffn1(nc, cst, A, x, n, ntab):
    ytab = nc.dram_tensor("ytab1", (S1 * P, C), F32, kind="Internal").ap()
    rtab = nc.dram_tensor("rtab1", (S1 * P, 1), F32, kind="Internal").ap()
    with ExitStack() as ctx:
        a = Pool_(nc, ctx, "ffn1")
        wt, pos = a.sb("wt", [P, NT]), a.sb("pos", [P, NT], I32)
        with ExitStack() as c1:
            b = Pool_(nc, c1, "ffn1g")
            w1, wg, bg = b.sb("w1", [P, KC, F1]), b.sb("wg", [P, FC1, E1]), b.sb("bg", [P, E1])
            logits, keys = b.sb("logits", [P, NT, E1]), b.sb("keys", [P, NT])
            experts, tokens = b.sb("experts", [1, S1], I32), b.sb("tokens", [P, S1], I32)
            b1t, b2b = b.sb("b1t", [P, 1, FC1]), b.sb("b2b", [P, E1, C])
            with ExitStack() as c2:
                load_biases(nc, Pool_(nc, c2, "bias1"), cst, A["L1_ffn_b1"].unsqueeze(0), b1t, A["L1_ffn_bd"], b2b)
            with ExitStack() as c2:
                gate_hidden(nc, Pool_(nc, c2, "hid1"), cst, A, n, w1, wg, bg, b1t, logits)
            gate(nc, "gate1", cst, logits, E1, keys, [wt[:]])
            route(nc, "route1", cst, keys, 1, E1, S1, 5, pos, experts, tokens, rtab)
            run_experts(nc, "exp1", cst, S1, experts, tokens, ntab, None, w1, b1t, True, FC1,
                        A["L1_ffn_Wd"], b2b, ACT.Gelu, ytab)
        with ExitStack() as c1:
            b = Pool_(nc, c1, "ffn1c")
            got = b.sb("got", [P, NT, C])
            fetch(nc, b, pos, NT, ytab, got)
            s_chain = b.sem("chain")
            with nc.Block() as block:

                @block.vector
                def _(dve):
                    link, V = Chain(dve, s_chain), nc.vector
                    link(V.tensor_tensor(got[:], got[:], bc(wt[:], 2, C), ALU.mult))
                    link(V.tensor_tensor(x[:], x[:], got[:], ALU.add))


def gate_hidden(nc, a, cst, A, n, w1, wg, bg, b1t, logits):
    TN = TB * P // 2
    xs, xt = a.sb("xs", [P, TB, C]), a.sb("xt", [P, KC, TB * P])
    ht = a.sb("ht", [P, FC1, 2, TN])
    turned = a.ps("turned", [P, TB + 1, C])
    hidden = a.ps("hidden", [P, 4, 512])
    out = a.ps("out", [P, 512])
    s_in, s_xs, s_turned, s_xt, s_hidden, s_ht, s_out, s_took = (
        a.sem(m) for m in ("in", "xs", "turned", "xt", "hidden", "ht", "out", "took"))
    with nc.Block() as block:

        @block.sync
        def _(sp):
            sp.dma_start(w1[:], A["L1_ffn_W1"].rearrange("(k p) f -> p k f", p=P)).then_inc(s_in, 16)
            sp.dma_start(wg[:], A["L1_ffn_Wg"].rearrange("(k p) e -> p k e", p=P)).then_inc(s_in, 16)
            row_broadcast(sp, bg[:], A["L1_ffn_bg"], s_in)

        @block.vector
        def _(dve):
            V = nc.vector
            dve.wait_ge(s_in, 48)
            V.tensor_copy(xs[:], n[:, 0:TB, :]).then_inc(s_xs, 1)
            with dve.Fori(0, TURNS - 1) as i:
                dve.wait_ge(s_turned, i + 1)
                V.tensor_copy(xs[:], n[:, bass.ds((i + 1) * TB, TB), :]).then_inc(s_xs, 1)
                dve.wait_ge(s_out, i + 1)
                V.tensor_tensor(logits[:, bass.ds(i * TB, TB), :], out[:, 0:TB * E1].rearrange("p (t e) -> p t e", e=E1),
                                bc(bg[:], 1, TB), ALU.add).then_inc(s_took, 1)
            dve.wait_ge(s_out, TURNS)
            V.tensor_tensor(logits[:, NT - TB:NT, :], out[:, 0:TB * E1].rearrange("p (t e) -> p t e", e=E1),
                            bc(bg[:], 1, TB), ALU.add).then_inc(s_took, 1)

        @block.tensor
        def _(pe):
            pe.wait_ge(s_in, 48)

            def turn(i, first=False):
                pe.wait_ge(s_xs, i + 1)
                for b in range(TB):
                    for k in range(KC):
                        last = nc.tensor.transpose(turned[:, b, k * P:(k + 1) * P], xs[:, b, k * P:(k + 1) * P],
                                                   cst["ident"][:])
                last.then_inc(s_turned, 1)
                pe.wait_ge(s_xt, i + 1)
                for f in range(FC1):
                    if not (first and f < 2):
                        pe.wait_ge(s_ht, i * FC1 + f - 1)
                    for m in range(2):
                        for k in range(KC):
                            last = nc.tensor.matmul(hidden[:, f % 2 * 2 + m, 0:TN], w1[:, k, f * P:(f + 1) * P],
                                                    xt[:, k, m * TN:(m + 1) * TN], start=(k == 0), stop=(k == KC - 1))
                    last.then_inc(s_hidden, 1)
                pe.wait_ge(s_ht, (i + 1) * FC1)
                if not first:
                    pe.wait_ge(s_took, i)
                for b in range(TB):
                    for f in range(FC1):
                        last = nc.tensor.matmul(out[:, b * E1:(b + 1) * E1],
                                                ht[:, f].rearrange("p m n -> p (m n)")[:, b * P:(b + 1) * P],
                                                wg[:, f, :], start=(f == 0), stop=(f == FC1 - 1))
                last.then_inc(s_out, 1)

            turn(0, first=True)
            with pe.Fori(1, TURNS) as i:
                turn(i)

        @block.scalar
        def _(act):
            def turn(i, first=False):
                act.wait_ge(s_turned, i + 1)
                nc.scalar.copy(xt[:].rearrange("p k (b n) -> p b k n", b=TB),
                               turned[:, 0:TB, :].rearrange("p b (k n) -> p b k n", k=KC)).then_inc(s_xt, 1)
                if not first:
                    act.wait_ge(s_out, i)
                for f in range(FC1):
                    act.wait_ge(s_hidden, i * FC1 + f + 1)
                    nc.scalar.activation(ht[:, f], hidden[:, f % 2 * 2:f % 2 * 2 + 2, 0:TN], ACT.Gelu,
                                         bias=b1t[:, 0, f:f + 1]).then_inc(s_ht, 1)

            turn(0, first=True)
            with act.Fori(1, TURNS) as i:
                turn(i)


def split(link, V, parts, rest, src):
    link(V.tensor_copy(parts[0], src))
    link(V.tensor_tensor(rest, src, parts[0], ALU.subtract))
    link(V.tensor_copy(parts[1], rest))
    link(V.tensor_tensor(rest, rest, parts[1], ALU.subtract))
    link(V.tensor_copy(parts[2], rest))


def heads_table(nc, cst, A, n, hparts, hdram):
    with ExitStack() as ctx:
        a = Pool_(nc, ctx, "heads")
        htab = a.sb("htab", [P, NT, HR + H])
        rest = a.sb("rest", [P, TB, HN])
        wn, wt = a.sb("wn", [P, KC, C]), a.sb("wt", [P, KC, C])
        av, tmp = a.sb("av", [P, 2, C]), a.sb("tmp", [P, TB, C])
        turned = a.ps("turned", [P, KC, C])
        s_in, s_turned, s_wt, s_chain, s_out, s_split = (a.sem(m) for m in ("in", "turned", "wt", "chain", "out", "split"))
        with nc.Block() as block:

            @block.sync
            def _(sp):
                sp.dma_start(wn[:], A["L1_gnn_W"].rearrange("(o p) c -> p o c", p=P)).then_inc(s_in, 16)
                row_broadcast(sp, av[:, 0, :], A["L1_gnn_a_src"].rearrange("h d -> (h d)"), s_in)
                row_broadcast(sp, av[:, 1, :], A["L1_gnn_a_dst"].rearrange("h d -> (h d)"), s_in)
                sp.wait_ge(s_in, 48)

            @block.tensor
            def _(pe):
                pe.wait_ge(s_in, 48)
                for k in range(KC):
                    for o in range(KC):
                        last = nc.tensor.transpose(turned[:, k, o * P:(o + 1) * P], wn[:, o, k * P:(k + 1) * P],
                                                   cst["ident"][:])
                last.then_inc(s_turned, 1)

            @block.scalar
            def _(act):
                act.wait_ge(s_turned, 1)
                nc.scalar.copy(wt[:], turned[:]).then_inc(s_wt, 1)

            @block.vector
            def _(dve):
                nc.vector.memset(htab[:], 1.0).then_inc(s_chain, 1)

        V = nc.vector

        def prep(link, i, xs):
            link(V.tensor_copy(xs[:], n[:, bass.ds(i * TB, TB), :]))

        def evac(link, i, ps):
            at = bass.ds(i * TB, TB)
            row = htab[:, at, 0:HW].rearrange("p t (h d) -> p t h d", d=D + 1)[:, :, :, 0:D]
            link(V.tensor_copy(row, ps[:, 0:TB, :].rearrange("p t (h d) -> p t h d", d=D)))
            for k in range(2):
                link(V.tensor_tensor(tmp[:], ps[:, 0:TB, :], bc(av[:, k, :], 1, TB), ALU.mult))
                link(V.tensor_reduce(htab[:, at, HW + k * H:HW + (k + 1) * H],
                                     tmp[:].rearrange("p t (h d) -> p t h d", d=D), AX, ALU.add))

        project(nc, "headsp", cst, wt, C, prep, 1, evac, 5)
        with nc.Block() as block:

            @block.sync
            def _(sp):
                sp.dma_start(hdram.rearrange("(t p) c -> p t c", p=P), htab[:, :, 0:HR]).then_inc(s_out, 16)
                sp.wait_ge(s_out, 16)

            @block.vector
            def _(dve):
                link = Chain(dve, s_split)
                for t in range(0, NT, TB):
                    at = slice(t, t + TB)
                    split(link, V, [hparts[:, at, k, 0:C].rearrange("p t (h d) -> p t h d", d=D) for k in range(3)],
                          rest[:, :, 0:C].rearrange("p t (h d) -> p t h d", d=D),
                          htab[:, at, 0:HW].rearrange("p t (h d) -> p t h d", d=D + 1)[:, :, :, 0:D])
                    split(link, V, [hparts[:, at, k, C:HN] for k in range(3)], rest[:, :, C:HN], htab[:, at, HR:HR + H])


def edge_weights(nc, a, A, cst, sorted1, ewz, fields):
    wn = a.sb("wn", [P, KC, 3])
    turned = a.ps("turned", [P, 512])
    enc, encb, rest = a.sb("enc", [4, C]), a.sb("encb", [4, 3, C], BF16), a.sb("rest", [4, C])
    left = a.sb("left", [P, NG * G, 3])
    s_in, s_bias, s_turned, s_enc, s_zero, s_split, s_out, s_chain = (
        a.sem(m) for m in ("in", "bias", "turned", "enc", "zero", "split", "out", "chain"))
    with nc.Block() as block:

        @block.gpsimd
        def _(pool):
            nc.gpsimd.memset(ewz[:], 0.0).then_inc(s_zero, 1)

        @block.vector
        def _(dve):
            link, V = Chain(dve, s_chain), nc.vector
            rec = sorted1[:].rearrange("p g (q r) -> p (g q) r", r=8)
            split(link, V, [fields[:, :, 3 * j:3 * j + 3] for j in range(3)], left[:], rec[:, :, 2:5])
            link(V.tensor_copy(fields[:, :, PF - 1], rec[:, :, 5]))
            dve.wait_ge(s_bias, 16)
            dve.wait_ge(s_enc, 1)
            split(link, V, [encb[:, i, :] for i in range(3)], rest[:], enc[:])
            dve.sem_inc(s_split, 1)

        @block.sync
        def _(sp):
            sp.dma_start(wn[:], A["L1_gnn_edge_W"].rearrange("(o p) c -> p o c", p=P)).then_inc(s_in, 16)
            sp.dma_start(enc[3:4, :], A["L1_gnn_edge_b"].unsqueeze(0)).then_inc(s_bias, 16)
            sp.wait_ge(s_zero, 1)
            sp.wait_ge(s_split, 1)
            for q in range(G):
                for i in range(3):
                    at = q * 32 + i * PF
                    for j in range(3):
                        sp.dma_start(ewz[at + 3 * j:at + 3 * j + 3, q, :], encb[0:3, i, :]).then_inc(s_out, 16)
                    sp.dma_start(ewz[at + 9:at + 10, q, :], encb[3:4, i, :]).then_inc(s_out, 16)
            sp.wait_ge(s_out, 16 * 12 * G)

        @block.tensor
        def _(pe):
            pe.wait_ge(s_in, 16)
            for o in range(KC):
                last = nc.tensor.transpose(turned[0:3, o * P:(o + 1) * P], wn[:, o, :], cst["ident"][:])
            last.then_inc(s_turned, 1)

        @block.scalar
        def _(act):
            act.wait_ge(s_turned, 1)
            nc.scalar.copy(enc[0:3, :], turned[0:3, 0:C]).then_inc(s_enc, 1)


def attention(nc, cst, A, sorted1, gb, hparts, hdram, acc):
    with ExitStack() as ctx:
        a = Pool_(nc, ctx, "att")
        two, four = range(2), range(4)
        ewz = a.sb("ewz", [P, G, C], BF16)
        fields = a.sb("fields", [P, NG * G, PF], BF16)
        top = a.sb("top", [P, NT, H])
        with ExitStack() as c1:
            edge_weights(nc, Pool_(nc, c1, "ew"), A, cst, sorted1, ewz, fields)
        ix = [a.sb(f"ix{s}", [P, G], I32) for s in four]
        rc = [a.sb(f"rc{s}", [P, G * 8]) for s in four]
        dist = a.sb("dist", [P, G, P])
        hot = [a.sb(f"hot{s}", [P, G, P]) for s in two]
        hotb = [a.sb(f"hotb{s}", [P, G, P], BF16) for s in four]
        hott = [a.sb(f"hott{s}", [P, G, P], BF16) for s in four]
        rcb = [a.sb(f"rcb{s}", [P, G, 32], BF16) for s in four]
        rct = [a.sb(f"rct{s}", [P, P], BF16) for s in four]
        rows = [a.sb(f"rows{s}", [P, G, HR]) for s in four]
        enc = a.sb("enc", [P, G, C])
        half = a.sb("half", [P, G * H, D // 2])
        al = [a.sb(f"al{s}", [P, G, H]) for s in four]
        alb = [a.sb(f"alb{s}", [P, 2, G * H], BF16) for s in four]
        line = a.sb("line", [G * H, 2, P])
        same, run = a.sb("same", [G * H, P + 1]), a.sb("run", [G * H, P])
        pen = a.sb("pen", [G * H, P])
        ends = a.sb("ends", [G * H, 2, P], BF16)
        back = a.sb("back", [P, 2, G * H], BF16)
        cand, gtop = a.sb("cand", [P, G, H]), a.sb("gtop", [P, H])
        ntop = a.sb("ntop", [P, H], BF16)
        fall = [a.sb(f"fall{s}", [P, H]) for s in two]
        dif = a.sb("dif", [P, G, H])
        ex = a.sb("ex", [P, G, H])
        msg = [a.sb(f"msg{s}", [P, G, HW]) for s in two]
        p_hot = a.ps("p_hot", [P, 2, G, P], BF16)
        p_h = a.ps("p_h", [P, G, C])
        p_z = a.ps("p_z", [P, G, C])
        p_small = a.ps("p_small", [P, 512])
        p_line = a.ps("p_line", [P, 1024], BF16)
        p_acc = a.ps("p_acc", [P, 512])
        a_line = p_line[0:G * H, 0:2 * P]
        a_back = p_line[:, 512:512 + 2 * G * H]
        a_adst = p_small[:, 320:320 + G * H]
        a_top = p_small[:, 192:192 + G * 2 * H]
        a_edge = p_small[:, 256:256 + G * H]
        sems = {m: a.sem(m) for m in ("chain", "ix", "hot", "p_hot", "hott", "hz", "al", "p_line", "line", "ends",
                                      "p_back", "back", "p_top", "ntop", "p_edge", "dif", "ex", "msg", "p_acc", "go",
                                      "fall", "took", "p_z", "enc", "go_pe", "hotb", "p_h", "prod", "half", "scale", "dist", "rc", "clear")}
        s_rows = [a.sem(f"rows{s}") for s in four]
        LOOPED = (NG - 5) // 4

        def ahead(eng, step):
            step(0, 0, 0)
            step(1, 1, 0)
            with eng.Fori(0, LOOPED) as i:
                for k in range(2, 6):
                    step(i * 4 + k, k, i)
            for g in range(4 * LOOPED + 2, NG):
                step(g, g % 4, g // 4)

        with nc.Block() as block:

            @block.gpsimd
            def _(pool):
                def halves(g):
                    pool.wait_ge(sems["prod"], g + 1)
                    e = enc[:].rearrange("p q (h k d) -> p (q h) k d", h=H, k=2)
                    nc.gpsimd.tensor_tensor(half[:], e[:, :, 0], e[:, :, 1], ALU.add).then_inc(sems["half"], 1)

                def messages(g, k, used=None):
                    pool.wait_ge(sems["ex"], g + 1)
                    if used is not None:
                        pool.wait_ge(sems["p_acc"], used)
                    nc.gpsimd.tensor_tensor(msg[k % 2][:].rearrange("p q (h d) -> p q h d", d=D + 1),
                                            rows[k % 4][:, :, 0:HW].rearrange("p q (h d) -> p q h d", d=D + 1),
                                            bc(ex[:], 3, D + 1), ALU.mult).then_inc(sems["msg"], 1)

                def gather(g, s):
                    pool.wait_ge(sems["ix"], g + 1)
                    pool.sem_inc(sems["go"], 1)
                    for q in range(G):
                        nc.gpsimd.indirect_dma_start(
                            rows[s][:, q, :], None, hdram,
                            bass.IndirectOffsetOnAxis(ap=ix[s][:, q:q + 1], axis=0)).then_inc(s_rows[s], 16)

                def step(g, k, i):
                    late = not isinstance(g, int)
                    if late or g + 3 < NG:
                        gather(g + 3, (k + 3) % 4)
                    messages(g, k, g - 1 if late or g > 1 else None)
                    if late or g + 2 < NG:
                        halves(g + 2)

                gather(0, 0)
                halves(0)
                gather(1, 1)
                halves(1)
                gather(2, 2)
                ahead(pool, step)

            @block.vector
            def _(dve):
                link, V = Chain(dve, sems["chain"]), nc.vector

                def products(g):
                    dve.wait_ge(sems["p_h"], g + 1)
                    dve.wait_ge(sems["enc"], g + 1)
                    V.tensor_tensor(enc[:], enc[:], p_h[:], ALU.mult).then_inc(sems["prod"], 1)

                def alphas(g, s, turn, edge=None):
                    dve.wait_ge(sems["half"], g + 1)
                    link(V.tensor_reduce(al[s][:].rearrange("p q h -> p (q h)"), half[:], AX, ALU.add))
                    dve.wait_ge(sems["hz"], g + 1)
                    if edge is not None:
                        dve.wait_ge(sems["p_edge"], edge)
                    link(V.tensor_tensor(al[s][:], al[s][:], a_adst.rearrange("p (q h) -> p q h", h=H), ALU.add))
                    dve.wait_ge(s_rows[s], turn * (16 * G))
                    link(V.tensor_tensor(al[s][:], al[s][:], rows[s][:, :, HW:HR], ALU.add))
                    link(V.scalar_tensor_tensor(al[s][:], al[s][:], 0.2, al[s][:], ALU.mult, ALU.max))
                    real = rc[s][:].rearrange("p (q r) -> p q r", r=8)[:, :, 5]
                    link(V.tensor_tensor(al[s][:], al[s][:], bc(real, 2, H), ALU.mult))
                    V.tensor_copy(alb[s][:, 0, :], al[s][:].rearrange("p q h -> p (q h)")).then_inc(sems["al"], 1)

                def segments(g):
                    dve.wait_ge(sems["line"], g + 1)
                    link(V.tensor_tensor(same[:, 1:P], line[:, 1, 1:P], line[:, 1, 0:P - 1], ALU.is_equal))
                    link(V.tensor_scalar(pen[:], same[:, 0:P], -1.0, BIG, ALU.add, ALU.mult))
                    link(V.tensor_tensor_scan(run[:], pen[:], line[:, 0, :], 0.0, ALU.add, ALU.max))
                    link(V.tensor_scalar(ends[:, 1, :], same[:, 1:P + 1], -1.0, 1.0, ALU.mult, ALU.add))
                    V.tensor_tensor(ends[:, 0, :], run[:], ends[:, 1, :], ALU.mult).then_inc(sems["ends"], 1)

                def maxima(g, s):
                    b = dve.value_load(gb[0:1, bass.ds(g, 1)], min_val=0, max_val=NT - 1)
                    dve.wait_ge(sems["p_top"], g + 1)
                    t = a_top.rearrange("p (q k h) -> p q k h", q=G, k=2)
                    link(V.tensor_scalar(cand[:], t[:, :, 1, :], -1.0, BIG, ALU.add, ALU.mult))
                    link(V.tensor_tensor(cand[:], cand[:], t[:, :, 0, :], ALU.add))
                    link(V.tensor_reduce(gtop[:], cand[:].rearrange("p q h -> p h q"), AX, ALU.max))
                    old = top[:, bass.ds(b, 1), :].rearrange("p a h -> p (a h)")
                    link(V.tensor_tensor(ntop[:], gtop[:], old, ALU.max))
                    dve.sem_inc(sems["ntop"], 1)
                    link(V.tensor_tensor(fall[s][:], old, ntop[:], ALU.subtract))
                    dve.sem_inc(sems["fall"], 1)
                    link(V.tensor_copy(old, ntop[:]))

                def exponents(g, s):
                    dve.wait_ge(sems["p_edge"], g + 1)
                    V.tensor_tensor(dif[:], al[s][:], a_edge.rearrange("p (q h) -> p q h", h=H),
                                    ALU.subtract).then_inc(sems["dif"], 1)

                def gathered(g, s):
                    b = dve.value_load(gb[0:1, bass.ds(g, 1)], min_val=0, max_val=NT - 1)
                    to = acc[:, bass.ds(b, 1), :].rearrange("p a (h d) -> p (a h) d", d=D + 1)
                    dve.wait_ge(sems["scale"], g + 1)
                    link(V.tensor_tensor(to, to, bc(fall[s][:], 2, D + 1), ALU.mult))
                    dve.wait_ge(sems["p_acc"], g + 1)
                    link(V.tensor_tensor(to, to, p_acc[:, 0:HW].rearrange("p (h d) -> p h d", d=D + 1), ALU.add))
                    dve.sem_inc(sems["took"], 1)

                def step(g, k, i):
                    late = not isinstance(g, int)
                    if late and k == 2:
                        link.turn(i, 4 * (6 + 5 + 4 + 2))
                    maxima(g, k % 2)
                    if late or g + 1 < NG:
                        alphas(g + 1, (k + 1) % 4, i + (k + 1) // 4 + 1, g + 1)
                    exponents(g, k % 4)
                    if late or g + 2 < NG:
                        products(g + 2)
                    if late or g + 1 < NG:
                        segments(g + 1)
                    if late or g > 0:
                        gathered(g - 1, (k + 1) % 2)
                    if late and k == 5:
                        link.end(LOOPED)

                for s in four:
                    V.memset(rcb[s][:], 0.0).then_inc(sems["clear"], 1)
                link(V.memset(acc[:], 0.0))
                link(V.memset(top[:], -BIG))
                link(V.memset(same[:], 0.0))
                products(0)
                alphas(0, 0, 1)
                segments(0)
                products(1)
                ahead(dve, step)
                gathered(NG - 1, (NG - 1) % 2)

            @block.tensor
            def _(pe):
                T = nc.tensor

                def lines(g, s):
                    pe.wait_ge(sems["al"], g + 1)
                    pe.sem_inc(sems["go_pe"], 1)
                    T.transpose(a_line[:, 0:P], alb[s][:, 0, :], cst["identb"][:])
                    T.transpose(a_line[:, P:2 * P], alb[s][:, 1, :], cst["identb"][:]).then_inc(sems["p_line"], 1)

                def backs(g):
                    pe.wait_ge(sems["ends"], g + 1)
                    pe.sem_inc(sems["go_pe"], 1)
                    for k in range(2):
                        last = T.transpose(a_back[:, k * G * H:(k + 1) * G * H], ends[:, k, :],
                                           cst["identb"][0:G * H, 0:G * H])
                    last.then_inc(sems["p_back"], 1)

                def turn_places(g, s):
                    pe.wait_ge(sems["hotb"], g + 1)
                    T.transpose(p_hot[:, 1, 0, :], rcb[s][:].rearrange("p q f -> p (q f)"), cst["identb"][:])
                    for q in range(G):
                        last = T.transpose(p_hot[:, 0, q, :], hotb[s][:, q, :], cst["identb"][:])
                    last.then_inc(sems["p_hot"], 1)

                def tops(g, s):
                    pe.wait_ge(sems["back"], g + 1)
                    for q in range(G):
                        last = T.matmul(a_top[:, q * 2 * H:(q + 1) * 2 * H].rearrange("p (k h) -> p k h", k=2),
                                        hotb[s][:, q, :], back[:, :, q * H:(q + 1) * H], start=True, stop=True)
                    last.then_inc(sems["p_top"], 1)

                def encoders(g, s):
                    pe.wait_ge(sems["hott"], g + 1)
                    for q in range(G):
                        last = T.matmul(p_z[:, q, :], rct[s][:], ewz[:, q, :], start=True, stop=True)
                    last.then_inc(sems["p_z"], 1)

                def destinations(g, s, between, first=False):
                    b = pe.value_load(gb[0:1, bass.ds(g, 1)], min_val=0, max_val=NT - 1)
                    if not first:
                        pe.wait_ge(sems["prod"], g)
                    node = hparts[:, bass.ds(b, 1), :, :].rearrange("p a k c -> p (a k) c")
                    for q in range(G):
                        for k in range(3):
                            last = T.matmul(p_h[:, q, :], hott[s][:, q, :], node[:, k, 0:C], start=(k == 0), stop=(k == 2))
                    last.then_inc(sems["p_h"], 1)
                    between()
                    for q in range(G):
                        for k in range(3):
                            last = T.matmul(a_adst[:, q * H:(q + 1) * H], hott[s][:, q, :], node[:, k, C:HN],
                                            start=(k == 0), stop=(k == 2))
                    last.then_inc(sems["hz"], 1)

                def edge_tops(g, s):
                    pe.wait_ge(sems["ntop"], g + 1)
                    for q in range(G):
                        last = T.matmul(a_edge[:, q * H:(q + 1) * H], hott[s][:, q, :], ntop[:], start=True, stop=True)
                    last.then_inc(sems["p_edge"], 1)

                def sums(g, k, first=False):
                    pe.wait_ge(sems["msg"], g + 1)
                    pe.wait_ge(sems["hot"], g + 1)
                    if not first:
                        pe.wait_ge(sems["took"], g)
                    for q in range(G):
                        last = T.matmul(p_acc[:, 0:HW], hot[k % 2][:, q, :], msg[k % 2][:, q, :], start=(q == 0), stop=(q == G - 1))
                    last.then_inc(sems["p_acc"], 1)

                def step(g, k, i):
                    late = not isinstance(g, int)
                    if late or g + 2 < NG:
                        turn_places(g + 2, (k + 2) % 4)
                    edge_tops(g, k % 4)
                    if late or g + 2 < NG:
                        encoders(g + 2, (k + 2) % 4)

                    def between():
                        if late or g + 1 < NG:
                            lines(g + 1, (k + 1) % 4)
                        pe.wait_ge(sems["dif"], g + 1)

                    if late or g + 2 < NG:
                        destinations(g + 2, (k + 2) % 4, between)
                    else:
                        between()
                    if late or g > 0:
                        sums(g - 1, k + 3, first=not late and g == 1)
                    if late or g + 1 < NG:
                        backs(g + 1)
                        tops(g + 1, (k + 1) % 4)

                turn_places(0, 0)
                encoders(0, 0)
                destinations(0, 0, lambda: None, first=True)
                turn_places(1, 1)
                encoders(1, 1)
                destinations(1, 1, lambda: lines(0, 0))
                backs(0)
                tops(0, 0)
                ahead(pe, step)
                sums(NG - 1, NG - 1)

            @block.scalar
            def _(act):
                S = nc.scalar

                def index(g, s):
                    r = sorted1[:, bass.ds(g, 1), :].rearrange("p a (q r) -> p (a q) r", r=8)
                    S.copy(ix[s][:], r[:, :, 0]).then_inc(sems["ix"], 1)

                def places(g, s):
                    r = sorted1[:, bass.ds(g, 1), :].rearrange("p a (q r) -> p (a q) r", r=8)
                    S.copy(rc[s][:], sorted1[:, bass.ds(g, 1), :].rearrange("p a x -> p (a x)")).then_inc(sems["rc"], 1)
                    S.copy(alb[s][:, 1, :].rearrange("p (q h) -> p q h", h=H), bc(r[:, :, 1], 2, H))
                    f = fields[:, bass.ds(g * G, G), :]
                    S.copy(rcb[s][:, :, 0:3 * PF].rearrange("p q (i f) -> p q i f", f=PF), bc(f, 2, 3))

                def distances(g, s):
                    act.wait_ge(sems["rc"], g + 1)
                    for q in range(G):
                        S.activation(dist[:, q, :], cst["iota"][:], ACT.Square, bias=rc[s][:, q * 8 + 1:q * 8 + 2],
                                     scale=-1.0).then_inc(sems["dist"], 1)

                def one_hot(g, s):
                    act.wait_ge(sems["dist"], g * G + G)
                    S.activation(hotb[s][:], dist[:], ACT.Relu, bias=cst["ones"][:, 0:1],
                                 scale=-1.0).then_inc(sems["hotb"], 1)

                def widen(g, k, used=None):
                    act.wait_ge(sems["hotb"], g + 1)
                    if used is not None:
                        act.wait_ge(sems["p_acc"], used)
                    S.copy(hot[k % 2][:], hotb[k % 4][:]).then_inc(sems["hot"], 1)

                def copy_turned(g, s):
                    act.wait_ge(sems["p_hot"], g + 1)
                    S.copy(rct[s][:], p_hot[:, 1, 0, :])
                    S.copy(hott[s][:], p_hot[:, 0]).then_inc(sems["hott"], 1)

                def encodings(g, first=False):
                    if not first:
                        act.wait_ge(sems["half"], g)
                    act.wait_ge(sems["p_z"], g + 1)
                    S.activation(enc[:], p_z[:], ACT.Relu).then_inc(sems["enc"], 1)

                def copy_lines(g):
                    act.wait_ge(sems["p_line"], g + 1)
                    S.copy(line[:], a_line.rearrange("p (k n) -> p k n", k=2)).then_inc(sems["line"], 1)

                def copy_back(g):
                    act.wait_ge(sems["p_back"], g + 1)
                    S.copy(back[:], a_back.rearrange("p (k n) -> p k n", k=2)).then_inc(sems["back"], 1)

                def step(g, k, i):
                    late = not isinstance(g, int)
                    if late or g + 2 < NG:
                        copy_turned(g + 2, (k + 2) % 4)
                    act.wait_ge(sems["fall"], g + 1)
                    S.activation(fall[k % 2][:], fall[k % 2][:], ACT.Exp).then_inc(sems["scale"], 1)
                    if late or g + 3 < NG:
                        places(g + 3, (k + 3) % 4)
                    if late or g + 2 < NG:
                        encodings(g + 2)
                    act.wait_ge(sems["dif"], g + 1)
                    S.activation(ex[:], dif[:], ACT.Exp).then_inc(sems["ex"], 1)
                    if late or g + 1 < NG:
                        copy_lines(g + 1)
                    if late or g + 3 < NG:
                        distances(g + 3, (k + 3) % 4)
                    if late or g + 1 < NG:
                        copy_back(g + 1)
                    if late or g + 3 < NG:
                        one_hot(g + 3, (k + 3) % 4)
                    widen(g, k, g - 1 if late or g > 1 else None)
                    act.wait_ge(sems["msg"], g + 1)
                    if late or g + 4 < NG:
                        index(g + 4, k % 4)

                act.wait_ge(sems["clear"], 4)
                for g in four:
                    index(g, g)
                for g in range(3):
                    places(g, g)
                    distances(g, g)
                    one_hot(g, g)
                copy_turned(0, 0)
                encodings(0, first=True)
                copy_turned(1, 1)
                encodings(1)
                copy_lines(0)
                copy_back(0)
                ahead(act, step)


def gnn1(nc, cst, A, x, n, sorted1, gb):
    hdram = nc.dram_tensor("hdram", (NPAD, HR), F32, kind="Internal").ap()
    with ExitStack() as ctx:
        a = Pool_(nc, ctx, "gnn1")
        hparts, acc = a.sb("hparts", [P, NT, 3, HN], BF16), a.sb("acc", [P, NT, HW])
        heads_table(nc, cst, A, n, hparts, hdram)
        attention(nc, cst, A, sorted1, gb, hparts, hdram, acc)
        bi, den = a.sb("bi", [P, C]), a.sb("den", [P, NT, H])
        s_in, s_chain = a.sem("in"), a.sem("chain")
        with nc.Block() as block:

            @block.sync
            def _(sp):
                row_broadcast(sp, bi[:], A["L1_gnn_bias"], s_in)

            @block.vector
            def _(dve):
                link, V = Chain(dve, s_chain), nc.vector
                out = acc[:].rearrange("p t (h d) -> p t h d", d=D + 1)
                link(V.tensor_scalar(den[:], out[:, :, :, D], 1e-10, None, ALU.max))
                link(V.reciprocal(den[:], den[:]))
                for t in range(0, NT, TB):
                    part = out[:, t:t + TB, :, 0:D]
                    to = x[:, t:t + TB, :]
                    link(V.tensor_tensor(part, part, bc(den[:, t:t + TB, :], 3, D), ALU.mult))
                    link(V.tensor_tensor(to.rearrange("p t (h d) -> p t h d", d=D),
                                         to.rearrange("p t (h d) -> p t h d", d=D), part, ALU.add))
                dve.wait_ge(s_in, 16)
                link(V.tensor_tensor(x[:], x[:], bc(bi[:], 1, NT), ALU.add))


def build(nc, A, out, debug=None):
    spent.clear()
    with ExitStack() as ctx:
        top = Pool_(nc, ctx, "top")
        cst = {n: top.sb(n, [P, P]) for n in ("iota", "lower", "ident", "ones")}
        cst["identb"] = top.sb("identb", [P, P], BF16)
        with ExitStack() as c1:
            constants(nc, Pool_(nc, c1, "const"), cst)
        sorted0, sorted1 = top.sb("sorted0", [P, NG, G * 4]), top.sb("sorted1", [P, NG, G * 8])
        gb = [top.sb(f"gb{k}", [1, NG], I32) for k in range(2)]
        tab0 = nc.dram_tensor("tab0", (NG * GE, 4), F32, kind="Internal").ap()
        tab1 = nc.dram_tensor("tab1", (E + GE, 8), F32, kind="Internal").ap()
        with ExitStack() as c1:
            a = Pool_(nc, c1, "edges")
            ek = [a.sb(f"key{k}", [P, EJ]) for k in range(2)]
            rec0, rec1 = a.sb("rec0", [P, EJ, 4]), a.sb("rec1", [P, EJ, 8])
            pos = [a.sb(f"pos{k}", [P, EJ], I32) for k in range(2)]
            bucket = a.sb("bucket", [P, NG])
            fill, unsorted = a.sb("fill", [P, NG, G * 4]), a.sb("unsorted", [1, 1], I32)
            with ExitStack() as c2:
                edge_keys(nc, Pool_(nc, c2, "keys"), A, cst, ek, rec0, rec1, unsorted)
            padding(nc, fill, tab1)
            order_edges(nc, cst, ek[1], rec1, tab1, pos[1], unsorted)
            sort_positions(nc, "sort0", cst, ek[0][:EP], EP, EJ, NT, GE, pos[0][:EP], NG, gb[0][:])
            load_groups(nc, cst, ek[1], tab1, sorted1[:], gb[1][:], bucket, lambda loads: scatter_rows(
                nc, "scat0", pos[0][:EP], rec0[:EP], tab0, EP, 25, 8,
                (tab0.rearrange("(p x) r -> p (x r)", p=P), fill[:].rearrange("p g x -> p (g x)")), sync_also=loads))
        with ExitStack() as c1:
            load_sorted(nc, Pool_(nc, c1, "back"), (tab0,), (sorted0,))
        if debug == "sort":
            return
        x, n = top.sb("x", [P, NT, C]), top.sb("n", [P, NT, C])
        ntab = nc.dram_tensor("ntab", (NPAD, C), F32, kind="Internal").ap()
        with ExitStack() as c1:
            load_nodes(nc, Pool_(nc, c1, "load"), A["x"], x)
        layernorm(nc, "ln0", x, n, ntab)
        with ExitStack() as c1:
            agg = Pool_(nc, c1, "agg").sb("agg", [P, NT, C])
            gather_sum(nc, cst, sorted0, gb[0], ntab, agg)
            gnn0(nc, cst, A, x, n, agg)
        if debug == "gnn0":
            with ExitStack() as c1:
                store_nodes(nc, Pool_(nc, c1, "store"), x, out)
            return
        layernorm(nc, "ln1", x, n, ntab)
        ffn0(nc, cst, A, x, n, ntab)
        if debug == "ffn0":
            with ExitStack() as c1:
                store_nodes(nc, Pool_(nc, c1, "store"), x, out)
            return
        reuse_semaphores(nc)
        layernorm(nc, "ln2", x, n)
        gnn1(nc, cst, A, x, n, sorted1, gb[1])
        if debug == "gnn1":
            with ExitStack() as c1:
                store_nodes(nc, Pool_(nc, c1, "store"), x, out)
            return
        reuse_semaphores(nc)
        layernorm(nc, "ln3", x, n, ntab)
        ffn1(nc, cst, A, x, n, ntab)
        with ExitStack() as c1:
            store_nodes(nc, Pool_(nc, c1, "store"), x, out)



def padding(nc, fill, tab1):
    s_chain, s_fill, s_tail = (nc.alloc_semaphore(f"pad_{m}") for m in ("chain", "fill", "tail"))
    with nc.Block() as block:

        @block.vector
        def _(dve):
            link = Chain(dve, s_chain)
            link(nc.vector.memset(fill[:], 0.0))
            r4 = fill[:].rearrange("p g (q r) -> p (g q) r", r=4)
            link(nc.vector.memset(r4[:, :, 1], -1.0))
            dve.sem_inc(s_fill, 1)

        @block.sync
        def _(sp):
            sp.wait_ge(s_fill, 1)
            rows = tab1[E:E + GE].rearrange("(p q) r -> p q r", p=P)
            of = fill[:].rearrange("p g (q r) -> p (g q) r", r=4)
            sp.dma_start(rows[:, :, 0:4], of[:, 0:G, :]).then_inc(s_tail, 16)
            sp.dma_start(rows[:, :, 4:6], of[:, 0:G, 2:4]).then_inc(s_tail, 16)
            sp.dma_start(rows[:, :, 6:8], of[:, 0:G, 2:4]).then_inc(s_tail, 16)
            sp.wait_ge(s_tail, 48)
    spent.extend((s_chain, s_fill, s_tail))


_INS = ['x', 'src', 'dst', 'edge_attr_3', 'edge_weight', 'L0_gnn_weight', 'L0_gnn_learnable_diag', 'L0_gnn_bias',
        'L0_ffn_gate_w', 'L0_ffn_gate_b', 'L0_ffn_w1', 'L0_ffn_b1', 'L0_ffn_w2', 'L0_ffn_b2', 'L0_ffn_gamma',
        'L0_ffn_beta', 'L1_gnn_W', 'L1_gnn_a_src', 'L1_gnn_a_dst', 'L1_gnn_edge_W', 'L1_gnn_edge_b', 'L1_gnn_bias',
        'L1_ffn_W1', 'L1_ffn_b1', 'L1_ffn_Wg', 'L1_ffn_bg', 'L1_ffn_Wd', 'L1_ffn_bd']
_OUT = ((N, C), 'float32')


def kernel(**inputs):
    import numpy as np
    import concourse.bacc as bacc
    from concourse.bass_utils import run_bass_kernel_spmd

    nc = bacc.Bacc("TRN2", target_bir_lowering=False, num_devices=1)
    arrays, args = {}, {}
    for name in _INS:
        a = np.ascontiguousarray(inputs[name])
        arrays[f"in_{name}"] = a
        args[name] = nc.dram_tensor(f"in_{name}", a.shape, mybir.dt.from_np(a.dtype), kind="ExternalInput").ap()
    out = nc.dram_tensor("out_dram", _OUT[0], F32, kind="ExternalOutput").ap()
    build(nc, args, out)
    r = run_bass_kernel_spmd(nc, [arrays], core_ids=[0])
    return r.results[0]["out_dram"]
```
